# Optimizing a Trainium2 kernel written in Bass

```python
import numpy as np
import jax
import jax.numpy as jnp

def _softmax(x, axis=-1):
    return jax.nn.softmax(x, axis=axis)

def _gelu(x):
    return jax.nn.gelu(x, approximate=True)

def _silu(x):
    return jax.nn.silu(x)

def _sigmoid(x):
    return jax.nn.sigmoid(x)

def _layernorm(x, axis=-1, eps=1e-05):
    m = jnp.mean(x, axis=axis, keepdims=True)
    v = jnp.var(x, axis=axis, keepdims=True)
    return (x - m) / jnp.sqrt(v + eps)

def _scatter_add(tgt, idx, src, axis=0):
    return tgt.at[idx].add(src)

def _segment_sum(src, seg, n):
    return jax.ops.segment_sum(src, seg, n)
kernel_name = 'mk_gnn_resnorm_d4_gnn_r16_0a25a1'

def setup_inputs(seed: int=0):
    np.random.seed(seed)
    _w = jnp.asarray

    def _rec_inputs():
        import jax
        import jax.numpy as jnp
        _gk = jax.random.key(seed)
        x = -0.0006008 + 1.001 * jax.random.normal(jax.random.fold_in(_gk, 1), (3125, 256), jnp.float32)
        _s = jax.random.randint(jax.random.fold_in(_gk, 2), (25000,), 0, 3125, jnp.int32)
        _d = jax.random.randint(jax.random.fold_in(_gk, 3), (25000,), 0, 3125, jnp.int32)
        _loop = jnp.arange(3125, dtype=jnp.int32)
        src = jnp.concatenate([_s, _d, _loop])
        dst = jnp.concatenate([_d, _s, _loop])
        _o = jnp.argsort(dst, stable=True)
        src = src[_o]
        dst = dst[_o]
        edge_type_3 = jax.random.randint(jax.random.fold_in(_gk, 13), (53125,), 0, 3, jnp.int32)
        edge_type_8 = jax.random.randint(jax.random.fold_in(_gk, 14), (53125,), 0, 8, jnp.int32)
        edge_weight = jax.random.uniform(jax.random.fold_in(_gk, 15), (53125,), jnp.float32, 0.0, 1)
        node_type_4 = jax.random.randint(jax.random.fold_in(_gk, 16), (3125,), 0, 4, jnp.int32)
        return (x, src, dst, edge_type_3, edge_type_8, edge_weight, node_type_4)
    x, src, dst, edge_type_3, edge_type_8, edge_weight, node_type_4 = _rec_inputs()

    def _L0_gnn_setup():
        import jax, jax.numpy as jnp
        import numpy as np
        N_NODES = 625
        N_EDGES = 20000
        D = 256
        key = jax.random.key(seed)
        k_x, k_w, k_m, k_s, k_d = jax.random.split(key, 5)
        x = jax.random.normal(k_x, (N_NODES, D), dtype=jnp.float32)
        W = jax.random.normal(k_w, (D, D), dtype=jnp.float32)
        M = jax.random.normal(k_m, (D, D), dtype=jnp.float32)
        edge_src = jax.random.randint(k_s, (N_EDGES,), 0, N_NODES, dtype=jnp.int64)
        edge_dst = jax.random.randint(k_d, (N_EDGES,), 0, N_NODES, dtype=jnp.int64)
        return {'x': x, 'W': W, 'M': M, 'edge_src': edge_src, 'edge_dst': edge_dst}
    _L0_gnn_all = _L0_gnn_setup()
    _L0_gnn_in = {k: v for k, v in _L0_gnn_all.items() if k in ('W', 'M')}
    del _L0_gnn_all

    def _L1_gnn_setup():
        import jax, jax.numpy as jnp
        import numpy as np
        N_NODES = 625
        N_EDGES = 20000
        FEA = 256
        HID = 256
        HEADS = 4
        ODIM = HID // HEADS
        NEG_SLOPE = 0.2

        def _gat_layer(x, W, al, ar, b, src, dst):
            n = x.shape[0]
            z = (x @ W).reshape(n, HEADS, ODIM)
            el = jnp.sum(z * al, axis=-1)
            er = jnp.sum(z * ar, axis=-1)
            e = jax.nn.leaky_relu(el[src] + er[dst], negative_slope=NEG_SLOPE)
            e_max = jax.ops.segment_max(e, dst, num_segments=n)
            ex = jnp.exp(e - e_max[dst])
            denom = jax.ops.segment_sum(ex, dst, num_segments=n)
            alpha = ex / denom[dst]
            msg = z[src] * alpha[:, :, None]
            out = jax.ops.segment_sum(msg, dst, num_segments=n)
            out = out + x.reshape(n, HEADS, ODIM)
            out = out + b.reshape(HEADS, ODIM)
            out = jax.nn.elu(out)
            return out.reshape(n, HID)
        key = jax.random.key(seed)
        ks = jax.random.split(key, 12)
        inp = {'features': jax.random.normal(ks[0], (N_NODES, FEA), dtype=jnp.float32), 'src': jax.random.randint(ks[1], (N_EDGES,), 0, N_NODES, dtype=jnp.int32), 'dst': jax.random.randint(ks[2], (N_EDGES,), 0, N_NODES, dtype=jnp.int32), 'W0': jax.random.normal(ks[3], (FEA, HID), dtype=jnp.float32) * (1.0 / np.sqrt(FEA)), 'al0': jax.random.normal(ks[4], (HEADS, ODIM), dtype=jnp.float32) * 0.1, 'ar0': jax.random.normal(ks[5], (HEADS, ODIM), dtype=jnp.float32) * 0.1, 'b0': jnp.zeros((HID,), dtype=jnp.float32), 'W1': jax.random.normal(ks[6], (HID, HID), dtype=jnp.float32) * (1.0 / np.sqrt(HID)), 'al1': jax.random.normal(ks[7], (HEADS, ODIM), dtype=jnp.float32) * 0.1, 'ar1': jax.random.normal(ks[8], (HEADS, ODIM), dtype=jnp.float32) * 0.1, 'b1': jnp.zeros((HID,), dtype=jnp.float32)}
        return inp
    _L1_gnn_all = _L1_gnn_setup()
    _L1_gnn_in = {k: v for k, v in _L1_gnn_all.items() if k in ('W0', 'al0', 'ar0', 'b0', 'W1', 'al1', 'ar1', 'b1')}
    del _L1_gnn_all

    def _L2_gnn_setup():
        import jax, jax.numpy as jnp
        import numpy as np
        import math
        L, H, HD, D = (3, 8, 32, 256)
        TN, TE = (4, 3)

        def _layer_norm(x, g, b, eps=1e-05):
            m = jnp.mean(x, axis=-1, keepdims=True)
            v = jnp.var(x, axis=-1, keepdims=True)
            return (x - m) / jnp.sqrt(v + eps) * g + b

        def _typed_transform(xh, W, types):
            out = jnp.zeros_like(xh)
            for t in range(W.shape[0]):
                y = jnp.einsum('mhd,hde->mhe', xh, W[t])
                out = jnp.where((types == t)[:, None, None], y, out)
            return out
        N, E = (1250, 20000)
        key = jax.random.key(seed)
        ks = jax.random.split(key, 16)
        inp = {}
        inp['x'] = jax.random.normal(ks[0], (N, D), dtype=jnp.float32)
        inp['edge_index'] = jax.random.randint(ks[1], (2, E), 0, N)
        inp['edge_type'] = jax.random.randint(ks[2], (E,), 0, TE)
        inp['node_type'] = jax.random.randint(ks[3], (N,), 0, TN)
        inp['W_Q'] = jax.random.normal(ks[4], (L, TN, H, HD, HD), dtype=jnp.float32) * 0.02
        inp['W_K'] = jax.random.normal(ks[5], (L, TN, H, HD, HD), dtype=jnp.float32) * 0.02
        inp['W_V'] = jax.random.normal(ks[6], (L, TN, H, HD, HD), dtype=jnp.float32) * 0.02
        inp['W_E'] = jax.random.normal(ks[7], (L, TE, H, HD, HD), dtype=jnp.float32) * 0.02
        inp['mu'] = jnp.ones((L, H, TE), dtype=jnp.float32)
        inp['Wo'] = jax.random.normal(ks[8], (L, D, D), dtype=jnp.float32) * 0.02
        inp['bo'] = jnp.zeros((L, D), dtype=jnp.float32)
        inp['ln1_g'] = jnp.ones((L, D), dtype=jnp.float32)
        inp['ln1_b'] = jnp.zeros((L, D), dtype=jnp.float32)
        inp['ln2_g'] = jnp.ones((L, D), dtype=jnp.float32)
        inp['ln2_b'] = jnp.zeros((L, D), dtype=jnp.float32)
        inp['w1'] = jax.random.normal(ks[9], (L, D, 4 * D), dtype=jnp.float32) * 0.02
        inp['b1'] = jnp.zeros((L, 4 * D), dtype=jnp.float32)
        inp['w2'] = jax.random.normal(ks[10], (L, 4 * D, D), dtype=jnp.float32) * 0.02
        inp['b2'] = jnp.zeros((L, D), dtype=jnp.float32)
        inp['out_g'] = jnp.ones((D,), dtype=jnp.float32)
        inp['out_b'] = jnp.zeros((D,), dtype=jnp.float32)
        return inp
    _L2_gnn_all = _L2_gnn_setup()
    _L2_gnn_in = {k: v for k, v in _L2_gnn_all.items() if k in ('W_Q', 'W_K', 'W_V', 'W_E', 'mu', 'Wo', 'bo', 'ln1_g', 'ln1_b', 'ln2_g', 'ln2_b', 'w1', 'b1', 'w2', 'b2', 'out_g', 'out_b')}
    del _L2_gnn_all

    def _L3_gnn_setup():
        import jax, jax.numpy as jnp
        import numpy as np
        N_NODES = 3125
        N_EDGES = 50000
        IN_FEAT = 256
        OUT_FEAT = 256
        NUM_RELS = 8
        NUM_BASES = 8
        SUBMAT_IN = IN_FEAT // NUM_BASES
        SUBMAT_OUT = OUT_FEAT // NUM_BASES
        key = jax.random.key(seed)
        k_h, k_w, k_src, k_dst, k_rel, k_norm = jax.random.split(key, 6)
        h = jax.random.normal(k_h, (N_NODES, IN_FEAT), dtype=jnp.float32)
        weight = jax.random.normal(k_w, (NUM_RELS, NUM_BASES * SUBMAT_IN * SUBMAT_OUT), dtype=jnp.float32) * 0.05
        edge_src = jax.random.randint(k_src, (N_EDGES,), 0, N_NODES, dtype=jnp.int32)
        edge_dst = jax.random.randint(k_dst, (N_EDGES,), 0, N_NODES, dtype=jnp.int32)
        edge_rel = jax.random.randint(k_rel, (N_EDGES,), 0, NUM_RELS, dtype=jnp.int32)
        edge_norm = jax.random.uniform(k_norm, (N_EDGES,), dtype=jnp.float32)
        return {'h': h, 'weight': weight, 'edge_src': edge_src, 'edge_dst': edge_dst, 'edge_rel': edge_rel, 'edge_norm': edge_norm}
    _L3_gnn_all = _L3_gnn_setup()
    _L3_gnn_in = {k: v for k, v in _L3_gnn_all.items() if k in ('weight',)}
    del _L3_gnn_all
    return {'x': x, 'src': src, 'dst': dst, 'edge_type_3': edge_type_3, 'edge_type_8': edge_type_8, 'edge_weight': edge_weight, 'node_type_4': node_type_4, 'L0_gnn_W': _L0_gnn_in['W'], 'L0_gnn_M': _L0_gnn_in['M'], 'L1_gnn_W0': _L1_gnn_in['W0'], 'L1_gnn_al0': _L1_gnn_in['al0'], 'L1_gnn_ar0': _L1_gnn_in['ar0'], 'L1_gnn_b0': _L1_gnn_in['b0'], 'L1_gnn_W1': _L1_gnn_in['W1'], 'L1_gnn_al1': _L1_gnn_in['al1'], 'L1_gnn_ar1': _L1_gnn_in['ar1'], 'L1_gnn_b1': _L1_gnn_in['b1'], 'L2_gnn_W_Q': _L2_gnn_in['W_Q'], 'L2_gnn_W_K': _L2_gnn_in['W_K'], 'L2_gnn_W_V': _L2_gnn_in['W_V'], 'L2_gnn_W_E': _L2_gnn_in['W_E'], 'L2_gnn_mu': _L2_gnn_in['mu'], 'L2_gnn_Wo': _L2_gnn_in['Wo'], 'L2_gnn_bo': _L2_gnn_in['bo'], 'L2_gnn_ln1_g': _L2_gnn_in['ln1_g'], 'L2_gnn_ln1_b': _L2_gnn_in['ln1_b'], 'L2_gnn_ln2_g': _L2_gnn_in['ln2_g'], 'L2_gnn_ln2_b': _L2_gnn_in['ln2_b'], 'L2_gnn_w1': _L2_gnn_in['w1'], 'L2_gnn_b1': _L2_gnn_in['b1'], 'L2_gnn_w2': _L2_gnn_in['w2'], 'L2_gnn_b2': _L2_gnn_in['b2'], 'L2_gnn_out_g': _L2_gnn_in['out_g'], 'L2_gnn_out_b': _L2_gnn_in['out_b'], 'L3_gnn_weight': _L3_gnn_in['weight']}

def reference(x, src, dst, edge_type_3, edge_type_8, edge_weight, node_type_4, L0_gnn_W, L0_gnn_M, L1_gnn_W0, L1_gnn_al0, L1_gnn_ar0, L1_gnn_b0, L1_gnn_W1, L1_gnn_al1, L1_gnn_ar1, L1_gnn_b1, L2_gnn_W_Q, L2_gnn_W_K, L2_gnn_W_V, L2_gnn_W_E, L2_gnn_mu, L2_gnn_Wo, L2_gnn_bo, L2_gnn_ln1_g, L2_gnn_ln1_b, L2_gnn_ln2_g, L2_gnn_ln2_b, L2_gnn_w1, L2_gnn_b1, L2_gnn_w2, L2_gnn_b2, L2_gnn_out_g, L2_gnn_out_b, L3_gnn_weight):
    import jax
    import jax.numpy as jnp

    def _L0_gnn_ref(x, W, M, edge_src, edge_dst):
        import jax, jax.numpy as jnp
        import numpy as np
        N_NODES = 625
        N_EDGES = 20000
        D = 256
        self_term = x @ W
        msg = x @ M
        agg = jax.ops.segment_sum(msg[edge_src], edge_dst, num_segments=x.shape[0])
        return jax.nn.relu(self_term + agg)

    def _L1_gnn_ref(features, src, dst, W0, al0, ar0, b0, W1, al1, ar1, b1):
        import jax, jax.numpy as jnp
        import numpy as np
        N_NODES = 625
        N_EDGES = 20000
        FEA = 256
        HID = 256
        HEADS = 4
        ODIM = HID // HEADS
        NEG_SLOPE = 0.2

        def _gat_layer(x, W, al, ar, b, src, dst):
            n = x.shape[0]
            z = (x @ W).reshape(n, HEADS, ODIM)
            el = jnp.sum(z * al, axis=-1)
            er = jnp.sum(z * ar, axis=-1)
            e = jax.nn.leaky_relu(el[src] + er[dst], negative_slope=NEG_SLOPE)
            e_max = jax.ops.segment_max(e, dst, num_segments=n)
            ex = jnp.exp(e - e_max[dst])
            denom = jax.ops.segment_sum(ex, dst, num_segments=n)
            alpha = ex / denom[dst]
            msg = z[src] * alpha[:, :, None]
            out = jax.ops.segment_sum(msg, dst, num_segments=n)
            out = out + x.reshape(n, HEADS, ODIM)
            out = out + b.reshape(HEADS, ODIM)
            out = jax.nn.elu(out)
            return out.reshape(n, HID)
        x = _gat_layer(features, W0, al0, ar0, b0, src, dst)
        x = _gat_layer(x, W1, al1, ar1, b1, src, dst)
        return x

    def _L2_gnn_ref(x, edge_index, edge_type, node_type, W_Q, W_K, W_V, W_E, mu, Wo, bo, ln1_g, ln1_b, ln2_g, ln2_b, w1, b1, w2, b2, out_g, out_b):
        import jax, jax.numpy as jnp
        import numpy as np
        import math
        L, H, HD, D = (3, 8, 32, 256)
        TN, TE = (4, 3)

        def _layer_norm(x, g, b, eps=1e-05):
            m = jnp.mean(x, axis=-1, keepdims=True)
            v = jnp.var(x, axis=-1, keepdims=True)
            return (x - m) / jnp.sqrt(v + eps) * g + b

        def _typed_transform(xh, W, types):
            out = jnp.zeros_like(xh)
            for t in range(W.shape[0]):
                y = jnp.einsum('mhd,hde->mhe', xh, W[t])
                out = jnp.where((types == t)[:, None, None], y, out)
            return out
        N = x.shape[0]
        src, dst = (edge_index[0], edge_index[1])
        scale = math.sqrt(HD)
        for l in range(L):
            xh = x.reshape(N, H, HD)
            Q = _typed_transform(xh, W_Q[l], node_type)
            K = _typed_transform(xh, W_K[l], node_type)
            V = _typed_transform(xh, W_V[l], node_type)
            q_dst = Q[dst]
            kt = _typed_transform(K[src], W_E[l], edge_type)
            scores = jnp.sum(q_dst * kt, axis=-1) / scale
            scores = scores * mu[l].T[edge_type]
            m = jax.ops.segment_max(scores, dst, num_segments=N)
            m = jnp.maximum(m, -1000000000.0)
            e = jnp.exp(scores - m[dst])
            s = jax.ops.segment_sum(e, dst, num_segments=N)
            w = e / (s[dst] + 1e-10)
            agg = jax.ops.segment_sum(V[src] * w[..., None], dst, num_segments=N)
            attn = agg.reshape(N, D) @ Wo[l] + bo[l]
            x = _layer_norm(x + attn, ln1_g[l], ln1_b[l])
            h = jax.nn.gelu(x @ w1[l] + b1[l], approximate=False) @ w2[l] + b2[l]
            x = _layer_norm(x + h, ln2_g[l], ln2_b[l])
        return _layer_norm(x, out_g, out_b)

    def _L3_gnn_ref(h, weight, edge_src, edge_dst, edge_rel, edge_norm):
        import jax, jax.numpy as jnp
        import numpy as np
        N_NODES = 3125
        N_EDGES = 50000
        IN_FEAT = 256
        OUT_FEAT = 256
        NUM_RELS = 8
        NUM_BASES = 8
        SUBMAT_IN = IN_FEAT // NUM_BASES
        SUBMAT_OUT = OUT_FEAT // NUM_BASES
        'RGCNBlockLayer forward (self_loop=False, bias=None, activation=None).\n\n            Per relation r: agg_r[v] = sum_{(u->v) in rel r} norm_e * h[u]\n            then block-diagonal matmul out_r = blockmm(agg_r, W_r); output = sum_r out_r.\n            '
        N, in_feat = h.shape
        R = weight.shape[0]
        msg = h[edge_src] * edge_norm[:, None]
        seg = edge_rel * N + edge_dst
        agg = jax.ops.segment_sum(msg, seg, num_segments=R * N)
        agg = agg.reshape(R, N, NUM_BASES, SUBMAT_IN)
        W = weight.reshape(R, NUM_BASES, SUBMAT_IN, SUBMAT_OUT)
        out = jnp.einsum('rnbi,rbio->nbo', agg, W)
        return out.reshape(N, NUM_BASES * SUBMAT_OUT)
    edge_index = jnp.stack([src, dst])
    x = _layernorm(x + _L0_gnn_ref(x, L0_gnn_W, L0_gnn_M, src, dst), axis=-1)
    x = _layernorm(x + _L1_gnn_ref(x, src, dst, L1_gnn_W0, L1_gnn_al0, L1_gnn_ar0, L1_gnn_b0, L1_gnn_W1, L1_gnn_al1, L1_gnn_ar1, L1_gnn_b1), axis=-1)
    x = _layernorm(x + _L2_gnn_ref(x, edge_index, edge_type_3, node_type_4, L2_gnn_W_Q, L2_gnn_W_K, L2_gnn_W_V, L2_gnn_W_E, L2_gnn_mu, L2_gnn_Wo, L2_gnn_bo, L2_gnn_ln1_g, L2_gnn_ln1_b, L2_gnn_ln2_g, L2_gnn_ln2_b, L2_gnn_w1, L2_gnn_b1, L2_gnn_w2, L2_gnn_b2, L2_gnn_out_g, L2_gnn_out_b), axis=-1)
    x = _layernorm(x + _L3_gnn_ref(x, L3_gnn_weight, src, dst, edge_type_8, edge_weight), axis=-1)
    return x

_drawn_inputs = setup_inputs


def setup_inputs(seed=0):
    import zlib

    import numpy as np

    out = dict(_drawn_inputs(seed))
    spreads = {'L1_gnn_b0': (0.0, 0.1),
     'L1_gnn_b1': (0.0, 0.1),
     'L2_gnn_mu': (1.0, 0.6),
     'L2_gnn_bo': (0.0, 0.1),
     'L2_gnn_ln1_g': (1.0, 0.2),
     'L2_gnn_ln1_b': (0.0, 0.1),
     'L2_gnn_ln2_g': (1.0, 0.2),
     'L2_gnn_ln2_b': (0.0, 0.1),
     'L2_gnn_b1': (0.0, 0.1),
     'L2_gnn_b2': (0.0, 0.1),
     'L2_gnn_out_g': (1.0, 0.2),
     'L2_gnn_out_b': (0.0, 0.1)}
    factors = {'L1_gnn_ar0': 2.948,
     'L1_gnn_ar1': 2.953,
     'L2_gnn_W_Q': 8.0,
     'L2_gnn_W_K': 8.0,
     'L2_gnn_W_V': 6.113,
     'L2_gnn_W_E': 8.0,
     'L2_gnn_Wo': 5.984}
    for name, (base, spread) in spreads.items():
        noise = np.random.default_rng([zlib.crc32(name.encode()), seed]).standard_normal(out[name].shape)
        drawn = base * np.exp(spread * noise) if base else spread * noise
        out[name] = jnp.asarray(drawn.astype(out[name].dtype))
    for name, factor in factors.items():
        out[name] = (out[name] * factor).astype(out[name].dtype)
    return out
```

```python
from contextlib import ExitStack, contextmanager

import numpy as np

import concourse.bass as bass
from concourse import mybir

F32 = mybir.dt.float32
BF16 = mybir.dt.bfloat16
I32 = mybir.dt.int32
ALU = mybir.AluOpType
ACT = mybir.ActivationFunctionType
AX = mybir.AxisListType

P = 128
N = 3125
D = 256
E = 53125
T = -(-N // P)
NP = T * P
TAIL = N - (T - 1) * P
HD = 8

EP, EJ = 125, 425
RG, RP = 5, 85
SORT_J = 17
NSORT = EJ // SORT_J

PAIRS = (E + 255 * T) // 256
PAIRS += -PAIRS % 8
CH = 2 * PAIRS
BODY = 8
NBODY = CH // BODY
HALF = NBODY // 2
GRP = P // HD
GB = CH // GRP
SL = GB * P
REC = 8
F_SRC, F_I3, F_I8, F_W, F_LO, F_DST = range(6)
LG, LP = 4, CH // 4
BIG = 1e30
EPS = 1e-5
W8 = D + HD
assert CH % GRP == 0 and NBODY % 2 == 0 and CH % LG == 0 and EP * EJ == E and CH <= 512
assert EJ == RG * RP and EJ % SORT_J == 0


class Link:

    def __init__(self, eng, sem, idle=None):
        self.idle = idle
        self.eng, self.sem, self.base, self.n, self.i, self.per = eng, sem, 0, 0, None, 0

    def do(self, ins):
        ins.then_inc(self.sem, 1)
        self.n += 1
        return self.n

    def wait(self, at=None):
        v = self.base + (self.n if at is None else at)
        self.eng.wait_ge(self.sem, v if self.i is None else self.i * self.per + v)

    def step(self, ins):
        self.do(ins)
        self.wait()

    def alone(self):
        self.eng.sem_inc(self.idle, 1)

    @contextmanager
    def loop(self, count, per):
        self.base, self.n = self.base + self.n, 0
        with self.eng.Fori(0, count) as i:
            self.i, self.per = i, per
            yield i
            assert self.n == per, (self.n, per)
        self.i, self.n = None, 0
        self.base += count * per


def build(nc, io):
    out = io["out"]
    rec = nc.dram_tensor("rec", (CH * P, REC), F32, kind="Internal").ap()
    tab_z = nc.dram_tensor("tab_z", (NP, D), F32, kind="Internal").ap()
    tab_e = nc.dram_tensor("tab_e", (NP, HD), F32, kind="Internal").ap()
    tab_k = nc.dram_tensor("tab_k", (3 * NP, D), F32, kind="Internal").ap()
    tab_v = nc.dram_tensor("tab_v", (NP, D), F32, kind="Internal").ap()
    tab_h = nc.dram_tensor("tab_h", (8 * NP, D), F32, kind="Internal").ap()

    outer = ExitStack()

    def keep(name, shape, dt=F32):
        return outer.enter_context(nc.sbuf_tensor(name, shape, dt))

    iota_row = keep("iota_row", [P, P])
    ident = keep("ident", [P, P])
    ident_b = keep("ident_b", [P, P], BF16)
    eps_c = keep("eps_c", [P, 1])
    X = keep("X", [P, T + 1, D])
    src_i = keep("src_i", [P, CH], I32)
    idx3_i = keep("idx3_i", [P, CH], I32)
    idx8_i = keep("idx8_i", [P, CH], I32)
    w_s = keep("w_s", [P, CH + BODY])
    lo_s = keep("lo_s", [P, CH + BODY])
    tile_q = keep("tile_q", [1, PAIRS], I32)

    @contextmanager
    def stage():
        with nc.cleanup_on_exit():
            with ExitStack() as st:
                class S:
                    def sb(self, name, shape, dt=F32):
                        return st.enter_context(nc.sbuf_tensor(nc.make_name(name, True), shape, dt))

                    def ps(self, name, shape, dt=F32):
                        return st.enter_context(nc.psum_tensor(nc.make_name(name, True), shape, dt))

                    def sem(self, name):
                        return nc.alloc_semaphore(nc.make_name(name, True))
                yield S()
        nc.all_engine_barrier()

    def steps(e, n, fn):
        with e.Fori(0, n // 2) as i:
            fn(i * 2, 0, i)
            fn(i * 2 + 1, 1, i)
        if n % 2:
            fn(n - 1, 0, n // 2)

    def bc(ap, axis, n):
        v = ap.unsqueeze(axis)
        shape = list(v.shape)
        shape[axis] = n
        return v.to_broadcast(shape)

    with stage() as s:
        s_x, s_c, s_z, s_i = s.sem("x"), s.sem("c"), s.sem("z"), s.sem("i")
        io_i = s.sb("io_i", [P, P], I32)
        with nc.Block() as blk:
            @blk.gpsimd
            def _(e):
                nc.gpsimd.iota(io_i[:, :], pattern=[[1, P]], base=0, channel_multiplier=0).then_inc(s_i, 1)
                nc.gpsimd.memset(ident[:, :], 0.0).then_inc(s_z, 1)
                e.wait_ge(s_z, 1)
                nc.gpsimd.affine_select(out=ident[:, :], in_=ident[:, :], compare_op=ALU.not_equal, fill=1.0,
                                        base=0, pattern=[[-1, P]], channel_multiplier=1).then_inc(s_c, 1)

            @blk.vector
            def _(e):
                nc.vector.memset(eps_c[:, :], EPS)
                nc.vector.memset(w_s[:, CH:], 0.0)
                nc.vector.memset(lo_s[:, CH:], -1.0)
                nc.vector.memset(X[:, T - 1:, :], 0.0).then_inc(s_x, 1)
                e.wait_ge(s_i, 1)
                nc.vector.tensor_copy(iota_row[:, :], io_i[:, :])
                e.wait_ge(s_c, 1)
                nc.vector.tensor_copy(ident_b[:, :], ident[:, :])

            @blk.sync
            def _(e):
                s_d = s.sem("d")
                e.dma_start(X[:, 0:T - 1, :], io["x"][0:(T - 1) * P, :].rearrange("(t p) d -> p t d", p=P)
                            ).then_inc(s_d, 16)
                e.wait_ge(s_x, 1)
                e.dma_start(X[0:TAIL, T - 1, :], io["x"][(T - 1) * P:N, :]).then_inc(s_d, 16)
                e.wait_ge(s_d, 32)

    with ExitStack() as sorting:
        def skeep(name, shape, dt=F32):
            return sorting.enter_context(nc.sbuf_tensor(name, shape, dt))
        R = skeep("R", [EP, EJ, REC])
        hi_c = skeep("hi_c", [EP, EJ])
        pos_i = skeep("pos_i", [EP, EJ], I32)
        oh_hi = skeep("oh_hi", [EP, EJ, T], BF16)
        pa = skeep("pa", [P, EJ, T], BF16)
        pb = skeep("pb", [P, EJ, T], BF16)
        counting = ExitStack()
        cnt = counting.enter_context(nc.sbuf_tensor("cnt", [P, T, EJ], F32))

        with stage() as s:
            rows_i = s.sb("rows_i", [RP, 4, RG * EP], I32)
            rows = s.sb("rows", [RP, 7, RG * EP])
            tmp_i = s.sb("tmp_i", [RP, 2, RG * EP], I32)
            pad = s.sb("pad", [P, CH * REC])
            ptr = [s.ps(f"ptr{k}", [EP, 512]) for k in range(7)]
            s_in, s_p, s_r, s_v, s_t, s_pad = (s.sem(n) for n in ("in", "p", "r", "v", "t", "pad"))
            with nc.Block() as blk:
                @blk.sync
                def _(e):
                    for k, name in enumerate(("src", "dst", "edge_type_3", "edge_type_8")):
                        e.dma_start(rows_i[:, k, :].rearrange("p (g e) -> p g e", g=RG),
                                    io[name].rearrange("(g p e) -> p g e", g=RG, p=RP)).then_inc(s_in, 16)
                    e.dma_start(rows[:, F_W, :].rearrange("p (g e) -> p g e", g=RG),
                                io["edge_weight"].rearrange("(g p e) -> p g e", g=RG, p=RP)).then_inc(s_in, 16)
                    e.wait_ge(s_p, 2)
                    e.dma_start(rec.rearrange("(p c) f -> p (c f)", p=P), pad[:, :]).then_inc(s_pad, 16)
                    e.wait_ge(s_pad, 16)

                @blk.vector
                def _(e):
                    L = Link(e, s_v)
                    nc.vector.memset(pad[:, :], 0.0).then_inc(s_p, 1)
                    e.wait_ge(s_p, 1)
                    nc.vector.memset(pad[:, :].rearrange("p (c f) -> p c f", f=REC)[:, :, F_LO:F_DST + 1], -1.0
                                     ).then_inc(s_p, 1)
                    L.do(nc.vector.memset(R[:, :, F_DST + 1:REC], 0.0))
                    e.wait_ge(s_in, 80)
                    L.do(nc.vector.tensor_copy(rows[:, F_SRC, :], rows_i[:, 0, :]))
                    L.do(nc.vector.tensor_copy(rows[:, F_DST, :], rows_i[:, 1, :]))
                    L.do(nc.vector.tensor_scalar(tmp_i[:, 0, :], rows_i[:, 1, :], 127, None, ALU.bitwise_and))
                    L.do(nc.vector.tensor_scalar(tmp_i[:, 1, :], rows_i[:, 1, :], 7, None, ALU.logical_shift_right))
                    L.wait()
                    L.do(nc.vector.tensor_copy(rows[:, F_LO, :], tmp_i[:, 0, :]))
                    L.do(nc.vector.tensor_copy(rows[:, 6, :], tmp_i[:, 1, :]))
                    for k, f in ((2, F_I3), (3, F_I8)):
                        L.do(nc.vector.scalar_tensor_tensor(rows[:, f, :], rows_i[:, k, :], float(NP),
                                                            rows[:, F_SRC, :], ALU.mult, ALU.add))
                    L.wait()
                    e.sem_inc(s_r, 1)
                    for f in range(7):
                        e.wait_ge(s_t, f + 1)
                        o = hi_c[:, :] if f == 6 else R[:, :, f]
                        L.do(nc.vector.tensor_copy(o, ptr[f][:, 0:EJ]))
                    L.wait()
                    L.step(nc.vector.tensor_tensor(oh_hi[:, :, :], bc(iota_row[0:EP, 0:T], 1, EJ), bc(hi_c[:, :], 2, T),
                                                   ALU.is_equal))

                @blk.tensor
                def _(e):
                    e.wait_ge(s_r, 1)
                    for f in range(7):
                        for g in range(RG):
                            last = nc.tensor.transpose(ptr[f][:, g * RP:(g + 1) * RP],
                                                       rows[:, f, g * EP:(g + 1) * EP], ident[0:RP, 0:RP])
                        last.then_inc(s_t, 1)

        with stage() as s:
            oh = s.sb("oh", [EP, SORT_J, P], BF16)
            pc = s.ps("pc", [P, 512])
            s_o, s_m, s_e = (s.sem(n) for n in ("o", "m", "e"))
            with nc.Block() as blk:
                @blk.vector
                def _(e):
                    e.sem_inc(s_m, 1)
                    with e.Fori(0, NSORT) as i:
                        e.wait_ge(s_m, i + 1)
                        nc.vector.tensor_tensor(oh[:, :, :], bc(iota_row[0:EP, :], 1, SORT_J),
                                                bc(R[:, bass.ds(i * SORT_J, SORT_J), F_LO], 2, P), ALU.is_equal
                                                ).then_inc(s_o, 1)

                @blk.tensor
                def _(e):
                    with e.Fori(0, NSORT) as i:
                        e.wait_ge(s_o, i + 1)
                        e.wait_ge(s_e, i + 1)
                        for k in range(SORT_J):
                            last = nc.tensor.matmul(pc[:, k * T:(k + 1) * T], oh[:, k, :],
                                                    oh_hi[:, bass.ds(i * SORT_J + k, 1), :].rearrange("p a t -> p (a t)"),
                                                    start=True, stop=True)
                        last.then_inc(s_m, 1)

                @blk.scalar
                def _(e):
                    e.sem_inc(s_e, 1)
                    with e.Fori(0, NSORT) as i:
                        e.wait_ge(s_m, i + 2)
                        nc.scalar.copy(cnt[:, :, bass.ds(i * SORT_J, SORT_J)],
                                       pc[:, 0:SORT_J * T].rearrange("p (j t) -> p t j", t=T)).then_inc(s_e, 1)

        with stage() as s:
            tot = s.sb("tot", [P, T])
            base = s.sb("base", [P, T])
            pairs_i = s.sb("pairs_i", [P, T], I32)
            pairs = s.sb("pairs", [P, T])
            pend = s.sb("pend", [P, T + 1])
            pref = s.sb("pref", [P, T, EJ])
            upper = s.sb("upper", [P, P])
            ones = s.sb("ones", [P, P])
            q_i = s.sb("q_i", [1, PAIRS], I32)
            q_f = s.sb("q_f", [1, PAIRS])
            q_ge = pref[0:1, :, :].rearrange("p t j -> p (t j)")[:, 0:PAIRS * T].rearrange("p (q t) -> p q t", t=T)
            pt = s.ps("pt", [P, 512])
            s_v, s_u, s_t, s_m = (s.sem(n) for n in ("v", "u", "t", "m"))
            with nc.Block() as blk:
                @blk.gpsimd
                def _(e):
                    nc.gpsimd.memset(upper[:, :], 1.0).then_inc(s_u, 1)
                    nc.gpsimd.memset(ones[:, :], 1.0).then_inc(s_u, 1)
                    nc.gpsimd.iota(q_i[:, :], pattern=[[1, PAIRS]], base=0, channel_multiplier=0).then_inc(s_u, 1)
                    e.wait_ge(s_u, 3)
                    nc.gpsimd.affine_select(out=upper[:, :], in_=upper[:, :], compare_op=ALU.is_gt, fill=0.0,
                                            base=0, pattern=[[1, P]], channel_multiplier=-1).then_inc(s_u, 1)

                @blk.tensor
                def _(e):
                    e.wait_ge(s_u, 4)
                    e.wait_ge(s_t, 1)
                    nc.tensor.matmul(pt[:, 0:T], upper[:, :], tot[:, :], start=True, stop=True)
                    nc.tensor.matmul(pt[:, T:2 * T], ones[:, :], tot[:, :], start=True, stop=True).then_inc(s_m, 1)

                @blk.vector
                def _(e):
                    L = Link(e, s_v)
                    nc.vector.tensor_reduce(tot[:, :], cnt[:, :, :], AX.X, ALU.add).then_inc(s_t, 1)
                    e.wait_ge(s_m, 1)
                    L.step(nc.vector.tensor_scalar(pairs_i[:, :], pt[:, T:2 * T], 255.0, None, ALU.add))
                    L.step(nc.vector.tensor_scalar(pairs_i[:, :], pairs_i[:, :], 8, None, ALU.logical_shift_right))
                    L.do(nc.vector.tensor_copy(pairs[:, :], pairs_i[:, :]))
                    L.do(nc.vector.memset(base[:, :], 0.0))
                    L.do(nc.vector.memset(pend[:, :], 0.0))
                    L.wait()
                    L.step(nc.vector.tensor_tensor_scan(pend[:, 1:T + 1], base[:, :], pairs[:, :], 0.0, ALU.add, ALU.add))
                    L.do(nc.vector.scalar_tensor_tensor(base[:, :], pend[:, 0:T], 256.0, pt[:, 0:T], ALU.mult, ALU.add))
                    e.wait_ge(s_u, 4)
                    L.do(nc.vector.tensor_copy(q_f[:, :], q_i[:, :]))
                    L.wait()
                    L.step(nc.vector.tensor_tensor(q_ge, bc(q_f[:, :], 2, T), bc(pend[0:1, 1:T + 1], 1, PAIRS), ALU.is_ge))
                    L.step(nc.vector.tensor_reduce(q_f[:, :], q_ge, AX.X, ALU.add))
                    L.do(nc.vector.tensor_scalar(tile_q[:, :], q_f[:, :], float(T - 1), None, ALU.min))
                    L.wait()
                    L.do(nc.vector.tensor_copy(pref[:, :, 0], base[:, :]))
                    for t in range(T):
                        L.do(nc.vector.tensor_tensor_scan(pref[:, t, 1:EJ], cnt[:, t, 0:EJ - 1], cnt[:, t, 0:EJ - 1],
                                                          base[:, t:t + 1], ALU.add, ALU.max))
                    L.wait()
                    L.step(nc.vector.tensor_copy(pa[:, :, :].rearrange("p j t -> p t j"), pref[:, :, :]))
                    L.step(nc.vector.tensor_tensor(pb[:, :, :].rearrange("p j t -> p t j"), pref[:, :, :],
                                                   pa[:, :, :].rearrange("p j t -> p t j"), ALU.subtract))

        counting.close()

        with stage() as s:
            drow = s.sb("drow", [EP, 2, SORT_J, EP], I32)
            oh = s.sb("oh", [EP, SORT_J, P], BF16)
            oht = s.sb("oht", [P, SORT_J, P], BF16)
            tri = s.sb("tri", [EP, EP])
            eq = s.sb("eq", [EP, SORT_J, EP], BF16)
            dcol = s.sb("dcol", [EP, SORT_J])
            same = s.sb("same", [EP, SORT_J])
            sel = s.sb("sel", [EP, SORT_J, T])
            spos = s.sb("spos", [EP, SORT_J])
            slot = s.sb("slot", [EP, 2, SORT_J], I32)
            recs = s.sb("recs", [EP, 2, SORT_J, REC])
            pt = [s.ps(f"pt{k}", [P, 8, P], BF16) for k in range(3)]
            pl = s.ps("pl", [EP, 512])
            s_tri, s_o, s_t, s_a, s_l, s_v, s_f, s_r, s_go, s_out = (
                s.sem(n) for n in ("tri", "o", "t", "a", "l", "v", "f", "r", "go", "out"))
            s_d = [s.sem("d0"), s.sem("d1")]
            s_s = [s.sem("s0"), s.sem("s1")]
            with nc.Block() as blk:
                @blk.sync
                def _(e):
                    def load(u, par, i):
                        e.wait_ge(s_f, u + 1)
                        e.dma_start(drow[:, par, :, :].rearrange("p j e -> p (j e)"),
                                    io["dst"][bass.ds(u * (SORT_J * EP), SORT_J * EP)].unsqueeze(0)
                                    .to_broadcast([EP, SORT_J * EP])).then_inc(s_d[par], 16)
                    steps(e, NSORT, load)

                @blk.tensor
                def _(e):
                    with e.Fori(0, NSORT) as i:
                        e.wait_ge(s_o, i + 1)
                        for k in range(SORT_J):
                            last = nc.tensor.transpose(pt[k // 8][:, k % 8, 0:EP], oh[:, k, :], ident_b[0:EP, 0:EP])
                        last.then_inc(s_t, 1)
                        e.wait_ge(s_a, i + 1)
                        e.wait_ge(s_f, i + 2)
                        for k in range(SORT_J):
                            for n, part in enumerate((pa, pb)):
                                last = nc.tensor.matmul(pl[:, k * T:(k + 1) * T], oht[:, k, 0:EP],
                                                        part[:, bass.ds(i * SORT_J + k, 1), :].rearrange("p a t -> p (a t)"),
                                                        start=(n == 0), stop=(n == 1))
                        last.then_inc(s_l, 1)

                @blk.scalar
                def _(e):
                    with e.Fori(0, NSORT) as i:
                        e.wait_ge(s_t, i + 1)
                        for k in range(3):
                            m = min(8, SORT_J - 8 * k)
                            last = nc.scalar.copy(oht[:, 8 * k:8 * k + m, 0:EP], pt[k][:, 0:m, 0:EP])
                        last.then_inc(s_a, 1)

                @blk.vector
                def _(e):
                    e.sem_inc(s_f, 2)
                    e.sem_inc(s_out, 2)
                    L = Link(e, s_v)
                    e.wait_ge(s_tri, 2)
                    per = 6 + SORT_J

                    def place(u, par, i):
                        L.i, L.per, L.n = u, per, 0
                        j0 = u * SORT_J
                        if par == 0 or True:
                            pass
                        e.wait_ge(s_t, u + 1 - 0) if False else None
                        L.do(nc.vector.tensor_copy(dcol[:, :], R[:, bass.ds(j0, SORT_J), F_DST]))
                        L.do(nc.vector.tensor_tensor(oh[:, :, :], bc(iota_row[0:EP, :], 1, SORT_J),
                                                     bc(R[:, bass.ds(j0, SORT_J), F_LO], 2, P), ALU.is_equal))
                        L.wait()
                        e.sem_inc(s_o, 1)
                        e.wait_ge(s_d[par], i * 16 + 16)
                        for k in range(SORT_J):
                            L.do(nc.vector.scalar_tensor_tensor(eq[:, k, :], drow[:, par, k, :], dcol[:, k:k + 1], tri[:, :],
                                                                ALU.is_equal, ALU.mult, accum_out=same[:, k:k + 1]))
                        e.wait_ge(s_l, u + 1)
                        L.step(nc.vector.tensor_tensor(sel[:, :, :], pl[:, 0:SORT_J * T].rearrange("p (j t) -> p j t", t=T),
                                                       oh_hi[:, bass.ds(j0, SORT_J), :], ALU.mult))
                        L.step(nc.vector.tensor_reduce(spos[:, :], sel[:, :, :], AX.X, ALU.add))
                        e.sem_inc(s_f, 1)
                        e.wait_ge(s_out, u + 1)
                        L.do(nc.vector.tensor_tensor(slot[:, par, :], spos[:, :], same[:, :], ALU.add))
                        L.do(nc.vector.tensor_copy(recs[:, par, :, :], R[:, bass.ds(j0, SORT_J), :]))
                        L.wait()
                        e.sem_inc(s_r, 1)
                        assert L.n == per, L.n
                    steps(e, NSORT, place)

                @blk.gpsimd
                def _(e):
                    nc.gpsimd.memset(tri[:, :], 1.0).then_inc(s_tri, 1)
                    e.wait_ge(s_tri, 1)
                    nc.gpsimd.affine_select(out=tri[:, :], in_=tri[:, :], compare_op=ALU.is_gt, fill=0.0, base=0,
                                            pattern=[[-1, EP]], channel_multiplier=1).then_inc(s_tri, 1)
                    per_step = 16 * SORT_J

                    def scatter(u, par):
                        e.wait_ge(s_r, u + 1)
                        e.sem_inc(s_go, 1)
                        for k in range(SORT_J):
                            nc.gpsimd.indirect_dma_start(
                                out=rec, out_offset=bass.IndirectOffsetOnAxis(ap=slot[:, par, k:k + 1], axis=0),
                                in_=recs[:, par, k, :], in_offset=None).then_inc(s_s[par], 16)

                    scatter(0, 0)
                    with e.Fori(0, NSORT // 2) as i:
                        scatter(i * 2 + 1, 1)
                        e.wait_ge(s_s[0], i * per_step + per_step)
                        e.sem_inc(s_out, 1)
                        scatter(i * 2 + 2, 0)
                        e.wait_ge(s_s[1], i * per_step + per_step)
                        e.sem_inc(s_out, 1)
                    e.wait_ge(s_s[0], per_step * ((NSORT + 1) // 2))

    H = keep("H", [P, T + 1, D])
    acc = keep("acc", [P, T + 1, W8])
    sc = keep("sc", [P, CH, HD])
    pen = keep("pen", [P, SL + 1])
    conn = keep("conn", [1, HD, GRP + 1])
    single = keep("single", [1, HD, GRP])
    scf = sc[:, :, :].rearrange("p (g b) h -> p b g h", g=GRP)

    def to_groups(e, ptr, last_sem, a):
        for b in range(GB):
            last = nc.tensor.transpose(ptr[b // 4][:, (b % 4) * P:(b % 4 + 1) * P], a[:, b * P:(b + 1) * P], ident[:, :])
            if b % 4 == 3 or b == GB - 1:
                last.then_inc(last_sem, 1)

    NBK = -(-GB // 4)

    def bank_w(k):
        return min(4, GB - 4 * k) * P

    with stage() as s:
        rt = s.sb("rt", [LP, LG, P * REC])
        dstc = s.sb("dstc", [P, CH])
        grp = s.sb("grp", [P, SL])
        ends = s.sb("ends", [P, 2])
        erow = s.sb("erow", [1, 2, P])
        ptr = [s.ps(f"ptr{k}", [P, 512]) for k in range(8)]
        s_in, s_t, s_v, s_x, s_g, s_y, s_r = (s.sem(n) for n in ("in", "t", "v", "x", "g", "y", "r"))
        with nc.Block() as blk:
            @blk.sync
            def _(e):
                e.dma_start(rt[:, :, :], rec.rearrange("(g p e) f -> p g (e f)", g=LG, p=LP)).then_inc(s_in, 16)
                e.wait_ge(s_in, 16)

            @blk.tensor
            def _(e):
                e.wait_ge(s_in, 16)
                for f in range(6):
                    for g in range(LG):
                        last = nc.tensor.transpose(ptr[f][:, g * LP:(g + 1) * LP],
                                                   rt[:, g, :].rearrange("p (e f) -> p f e", f=REC)[:, f, :],
                                                   ident[0:LP, 0:LP])
                    last.then_inc(s_t, 1)
                e.wait_ge(s_x, 1)
                to_groups(e, ptr, s_g, sc[:, :, :].rearrange("p c h -> p (c h)"))
                e.wait_ge(s_y, 1)
                for k in range(2):
                    last = nc.tensor.transpose(ptr[0][0:1, k * P:(k + 1) * P], ends[:, k:k + 1], ident[:, :])
                last.then_inc(s_r, 1)

            @blk.vector
            def _(e):
                L = Link(e, s_v)
                L.do(nc.vector.memset(H[:, T - 1:, :], 0.0))
                L.do(nc.vector.memset(acc[:, T:, :], 0.0))
                L.do(nc.vector.memset(pen[:, :], 0.0))
                L.do(nc.vector.memset(conn[:, :, :], -BIG))
                for f, o in enumerate((src_i, idx3_i, idx8_i, w_s, lo_s, dstc)):
                    e.wait_ge(s_t, f + 1)
                    L.do(nc.vector.tensor_copy(o[:, 0:CH], ptr[f][:, 0:CH]))
                L.wait()
                L.step(nc.vector.tensor_copy(sc[:, :, :].rearrange("p c h -> p (c h)").rearrange("p (b g h) -> p b g h", g=GRP, h=HD),
                                             bc(dstc[:, :].rearrange("p (g b) -> p b g", g=GRP), 3, HD)))
                e.sem_inc(s_x, 1)
                for k in range(NBK):
                    e.wait_ge(s_g, k + 1)
                    L.do(nc.vector.tensor_copy(grp[:, k * 512:k * 512 + bank_w(k)], ptr[k][:, 0:bank_w(k)]))
                L.wait()
                L.do(nc.vector.tensor_copy(ends[:, 0:1], grp[:, 0:1]))
                L.do(nc.vector.tensor_copy(ends[:, 1:2], grp[:, SL - 1:SL]))
                L.wait()
                e.sem_inc(s_y, 1)
                L.step(nc.vector.tensor_tensor(pen[:, 1:SL], grp[:, 0:SL - 1], grp[:, 1:SL], ALU.not_equal))
                L.do(nc.vector.tensor_scalar(pen[:, 1:SL], pen[:, 1:SL], -BIG, None, ALU.mult))
                e.wait_ge(s_r, 1)
                L.step(nc.vector.tensor_copy(erow[:, :, :], ptr[0][0:1, 0:2 * P].rearrange("o (k x) -> o k x", k=2)))
                first = erow[:, 0, :].rearrange("o (g h) -> o h g", h=HD)
                lastd = erow[:, 1, :].rearrange("o (g h) -> o h g", h=HD)
                L.do(nc.vector.tensor_tensor(conn[:, :, 1:GRP], lastd[:, :, 0:GRP - 1], first[:, :, 1:GRP], ALU.not_equal))
                L.do(nc.vector.tensor_tensor(single[:, :, :], lastd, first, ALU.not_equal))
                L.wait()
                L.do(nc.vector.tensor_scalar(conn[:, :, 1:GRP], conn[:, :, 1:GRP], -BIG, None, ALU.mult))
                L.do(nc.vector.tensor_scalar(single[:, :, :], single[:, :, :], -BIG, None, ALU.mult))
                L.wait()

    def softmax():
        with stage() as s:
            S1 = s.sb("S1", [P, SL])
            F = s.sb("F", [P, SL])
            M = s.sb("M", [P, SL])
            penc = s.sb("penc", [1, 2, HD, GRP])
            frow = s.sb("frow", [1, HD, GRP])
            crow = s.sb("crow", [1, HD, GRP])
            cin = s.sb("cin", [1, GRP, HD])
            carry = s.sb("carry", [P, 1])
            ptr = [s.ps(f"ptr{k}", [P, 512]) for k in range(8)]
            Mg = M[:, :].rearrange("p (b g h) -> p b g h", g=GRP, h=HD)
            s_pm, s_pa, s_g, s_v, s_f, s_r, s_c, s_cc, s_sub, s_e, s_b, s_w, s_a = (
                s.sem(n) for n in ("pm", "pa", "g", "v", "f", "r", "c", "cc", "sub", "e", "b", "w", "a"))
            with nc.Block() as blk:
                @blk.tensor
                def _(e):
                    e.wait_ge(s_pm, 1)
                    e.wait_ge(s_pa, 1)
                    to_groups(e, ptr, s_g, M)
                    for k in range(2):
                        e.wait_ge(s_f, k + 1)
                        nc.tensor.transpose(ptr[0][0:1, 0:P], (F[:, SL - 1:SL], M[:, 0:1])[k], ident[:, :]).then_inc(s_r, 1)
                        e.wait_ge(s_c, k + 1)
                        nc.tensor.transpose(ptr[1][:, 0:1], cin[:, :, :].rearrange("o g h -> o (g h)"), ident[0:1, 0:1]
                                            ).then_inc(s_cc, 1)
                    for b in range(GB):
                        if b % 4 == 0:
                            e.wait_ge(s_e, b // 4 + 1)
                        last = nc.tensor.transpose(ptr[b // 4][:, (b % 4) * P:(b % 4 + 1) * P], S1[:, b * P:(b + 1) * P],
                                                   ident[:, :])
                        if b % 4 == 3 or b == GB - 1:
                            last.then_inc(s_b, 1)

                @blk.scalar
                def _(e):
                    nc.scalar.copy(Mg[:, GB // 2:, :, :], scf[:, GB // 2:, :, :]).then_inc(s_pa, 1)
                    for k in range(0, NBK, 2):
                        e.wait_ge(s_g, k + 1)
                        nc.scalar.copy(S1[:, k * 512:k * 512 + bank_w(k)], ptr[k][:, 0:bank_w(k)]).then_inc(s_a, 1)
                    for k in range(NBK):
                        e.wait_ge(s_sub, k + 1)
                        sl = slice(k * 512, k * 512 + bank_w(k))
                        nc.scalar.activation(S1[:, sl], S1[:, sl], ACT.Exp).then_inc(s_e, 1)
                    for k in range(0, NBK, 2):
                        e.wait_ge(s_b, k + 1)
                        n = bank_w(k) // P
                        nc.scalar.copy(scf[:, 4 * k:4 * k + n, :, :],
                                       ptr[k][:, 0:n * P].rearrange("p (b g h) -> p b g h", b=n, h=HD)).then_inc(s_w, 1)

                @blk.vector
                def _(e):
                    L = Link(e, s_v)
                    nc.vector.tensor_copy(Mg[:, 0:GB // 2, :, :], scf[:, 0:GB // 2, :, :]).then_inc(s_pm, 1)
                    L.do(nc.vector.tensor_tensor(penc[:, 0, :, :], conn[:, :, 0:GRP], single[:, :, :], ALU.add))
                    L.do(nc.vector.tensor_tensor(penc[:, 1, :, :], conn[:, :, 1:GRP + 1], single[:, :, :], ALU.add))
                    L.do(nc.vector.memset(cin[:, :, :], -BIG))
                    for k in range(1, NBK, 2):
                        e.wait_ge(s_g, k + 1)
                        L.do(nc.vector.tensor_copy(S1[:, k * 512:k * 512 + bank_w(k)], ptr[k][:, 0:bank_w(k)]))
                    L.wait()
                    e.wait_ge(s_a, (NBK + 1) // 2)
                    flat = lambda a: a.rearrange("o h g -> o (h g)")
                    for k in range(2):
                        if k == 0:
                            out_, pen_, in_ = F[:, :], pen[:, 0:SL], S1[:, :]
                        else:
                            out_, pen_, in_ = M[:, ::-1], pen[:, 1:SL + 1][:, ::-1], F[:, ::-1]
                        L.step(nc.vector.tensor_tensor_scan(out_, pen_, in_, -BIG, ALU.add, ALU.max))
                        e.sem_inc(s_f, 1)
                        e.wait_ge(s_r, k + 1)
                        L.step(nc.vector.tensor_copy(frow[:, :, :], ptr[0][0:1, 0:P].rearrange("o (g h) -> o h g", h=HD)))
                        d = slice(None) if k == 0 else slice(None, None, -1)
                        L.step(nc.vector.tensor_tensor_scan(flat(crow[:, :, :])[:, d], flat(penc[:, k, :, :])[:, d],
                                                            flat(frow[:, :, :])[:, d], -BIG, ALU.add, ALU.max))
                        cv = cin[:, :, :].rearrange("o g h -> o h g")
                        if k == 0:
                            L.step(nc.vector.tensor_tensor(cv[:, :, 1:GRP], crow[:, :, 0:GRP - 1], conn[:, :, 1:GRP], ALU.add))
                        else:
                            L.do(nc.vector.memset(cin[:, GRP - 1, :], -BIG))
                            L.do(nc.vector.tensor_tensor(cv[:, :, 0:GRP - 1], crow[:, :, 1:GRP], conn[:, :, 1:GRP], ALU.add))
                            L.wait()
                        e.sem_inc(s_c, 1)
                        e.wait_ge(s_cc, k + 1)
                        L.step(nc.vector.tensor_copy(carry[:, :], ptr[1][:, 0:1]))
                        L.step(nc.vector.tensor_tensor_scan(out_, pen_, in_, carry[:, :], ALU.add, ALU.max))
                    for k in range(NBK):
                        sl = slice(k * 512, k * 512 + bank_w(k))
                        nc.vector.tensor_tensor(S1[:, sl], S1[:, sl], M[:, sl], ALU.subtract).then_inc(s_sub, 1)
                    for k in range(1, NBK, 2):
                        e.wait_ge(s_b, k + 1)
                        n = bank_w(k) // P
                        nc.vector.tensor_copy(scf[:, 4 * k:4 * k + n, :, :],
                                              ptr[k][:, 0:n * P].rearrange("p (b g h) -> p b g h", b=n, h=HD)).then_inc(s_w, 1)

    def gather(e, ring, islot, idx, table, s_free, s_is, s_go, s_g):
        def step(u, par, i):
            e.wait_ge(s_free, u + 1)
            e.sem_inc(s_go, 1)
            nc.gpsimd.tensor_copy(islot[:, par, :], idx[:, bass.ds(u * BODY, BODY)]).then_inc(s_is, 1)
            e.wait_ge(s_is, u + 1)
            e.sem_inc(s_go, 1)
            for k in range(BODY):
                nc.gpsimd.indirect_dma_start(
                    out=ring[:, par, k, :], out_offset=None, in_=table,
                    in_offset=bass.IndirectOffsetOnAxis(ap=islot[:, par, k:k + 1], axis=0)).then_inc(s_g[par], 16)
        steps(e, NBODY, step)

    def tiles_of(e_type, u):
        _, vals = nc.values_load_multi_w_load_instructions(
            tile_q[0:1, bass.ds(u * (BODY // 2), BODY // 2)], engines=[e_type], min_val=0, max_val=T - 1,
            skip_runtime_bounds_check_because="they come from a minimum with T - 1")
        return vals

    def score_edges(Qs, width, idx, table, lrelu):
        with stage() as s:
            ring = s.sb("ring", [P, 2, BODY, width])
            islot = s.sb("islot", [P, 2, BODY], I32)
            oh = s.sb("oh", [P, 2, BODY, P], BF16)
            oht = s.sb("oht", [P, BODY, P], BF16)
            prod = s.sb("prod", [P, 4, 2, width]) if width == D else None
            pr8 = s.sb("pr8", [P, BODY, HD])
            pt = s.ps("pt", [P, BODY, P], BF16)
            nq = 4 if width == D else 2
            pq = [s.ps(f"pq{k}", [P, 512]) for k in range(nq)]
            s_free, s_is, s_go, s_oh, s_tr, s_ev, s_q, s_qf, s_v = (
                s.sem(n) for n in ("free", "is", "go", "oh", "tr", "ev", "q", "qf", "v"))
            s_g = [s.sem("g0"), s.sem("g1")]
            with nc.Block() as blk:
                @blk.gpsimd
                def _(e):
                    gather(e, ring, islot, idx, table, s_free, s_is, s_go, s_g)

                @blk.tensor
                def _(e):
                    e.sem_inc(s_tr, 2)

                    def step(u, par, i):
                        tl = tiles_of(mybir.EngineType.PE, u)
                        e.wait_ge(s_oh, u + 1)
                        for k in range(BODY):
                            last = nc.tensor.transpose(pt[:, k, :], oh[:, par, k, :], ident_b[:, :])
                        last.then_inc(s_tr, 1)
                        e.wait_ge(s_ev, u + 1)
                        for k in range(BODY // 2):
                            if width == D:
                                e.wait_ge(s_qf, u * 4 + (k + 1))
                                bank = pq[k]
                            else:
                                if k == 0:
                                    e.wait_ge(s_qf, u + 1)
                                bank = pq[par]
                            for c in range(2):
                                at = c * D if width == D else (2 * k + c) * width
                                for r in range(3):
                                    last = nc.tensor.matmul(bank[:, at:at + width], oht[:, 2 * k + c, :],
                                                            Qs[:, bass.ds(tl[k], 1), r, :].rearrange("p a d -> p (a d)"),
                                                            start=(r == 0), stop=(r == 2))
                            if width == D or k == BODY // 2 - 1:
                                last.then_inc(s_q, 1)
                    steps(e, NBODY, step)

                @blk.scalar
                def _(e):
                    with e.Fori(0, NBODY) as i:
                        e.wait_ge(s_tr, i + 3)
                        nc.scalar.copy(oht[:, :, :], pt[:, :, :]).then_inc(s_ev, 1)

                @blk.vector
                def _(e):
                    L = Link(e, s_v)
                    e.sem_inc(s_free, 2)
                    e.sem_inc(s_qf, 4 if width == D else 2)

                    def onehot(u, par):
                        e.wait_ge(s_tr, u + 1)
                        nc.vector.tensor_tensor(oh[:, par, :, :], bc(iota_row[:, :], 1, BODY),
                                                bc(lo_s[:, bass.ds(u * BODY, BODY)], 2, P), ALU.is_equal).then_inc(s_oh, 1)

                    e.wait_ge(s_tr, 1)
                    nc.vector.tensor_tensor(oh[:, 0, :, :], bc(iota_row[:, :], 1, BODY), bc(lo_s[:, 0:BODY], 2, P),
                                            ALU.is_equal).then_inc(s_oh, 1)
                    per = 8 if width == D else 2

                    def step(u, par, i):
                        onehot(u + 1, 1 - par)
                        e.wait_ge(s_g[par], i * (16 * BODY) + 16 * BODY)
                        L.i, L.per, L.n = u, per, 0
                        if width == D:
                            def mul(k):
                                e.wait_ge(s_q, u * 4 + (k + 1))
                                L.do(nc.vector.tensor_tensor(prod[:, k, :, :], ring[:, par, 2 * k:2 * k + 2, :],
                                                             pq[k][:, :].rearrange("p (c d) -> p c d", c=2), ALU.mult))
                                return L.n

                            def add(k, at):
                                L.wait(at)
                                L.do(nc.vector.tensor_reduce(
                                    sc[:, bass.ds(u * BODY + 2 * k, 2), :],
                                    prod[:, k, :, :].rearrange("p c (h x) -> p c h x", h=HD), AX.X, ALU.add))
                            at = mul(0)
                            for k in range(1, 4):
                                nxt = mul(k)
                                add(k - 1, at)
                                at = nxt
                            add(3, at)
                            L.wait()
                            e.sem_inc(s_qf, 4)
                        else:
                            e.wait_ge(s_q, u + 1)
                            o = sc[:, bass.ds(u * BODY, BODY), :]
                            L.step(nc.vector.tensor_tensor(pr8[:, :, :], ring[:, par, :, :], pq[par][:, 0:BODY * width].rearrange("p (c x) -> p c x", c=BODY), ALU.add))
                            L.step(nc.vector.scalar_tensor_tensor(o, pr8[:, :, :], 0.2, pr8[:, :, :], ALU.mult, ALU.max))
                            e.sem_inc(s_qf, 1)
                        e.sem_inc(s_free, 1)
                    steps(e, NBODY, step)

    def sum_edges(idx, table, mode):
        heads = mode if isinstance(mode, int) else 0
        wid = W8 if heads else D
        with stage() as s:
            ring = s.sb("ring", [P, 2, BODY, D])
            islot = s.sb("islot", [P, 2, BODY], I32)
            oh = s.sb("oh", [P, 2, BODY, P])
            val = s.sb("val", [P, 2, BODY, W8]) if heads else ring
            pp = [s.ps(f"pp{k}", [P, 512]) for k in range(4)]
            s_free, s_is, s_go, s_oh, s_ohf, s_val, s_ex, s_p, s_pf, s_v, s_v2 = (
                s.sem(n) for n in ("free", "is", "go", "oh", "ohf", "val", "ex", "p", "pf", "v", "v2"))
            s_g = [s.sem("g0"), s.sem("g1")]
            with nc.Block() as blk:
                @blk.gpsimd
                def _(e):
                    gather(e, ring, islot, idx, table, s_free, s_is, s_go, s_g)

                @blk.tensor
                def _(e):
                    e.sem_inc(s_ohf, 2)
                    if not heads:
                        e.sem_inc(s_free, 2)

                    def step(u, par, i):
                        e.wait_ge(s_oh, u + 1)
                        if heads:
                            e.wait_ge(s_ex, u + 1)
                        else:
                            e.wait_ge(s_g[par], i * (16 * BODY) + 16 * BODY)
                        for k in range(BODY // 2):
                            if heads:
                                e.wait_ge(s_val, u * 4 + (k + 1))
                            e.wait_ge(s_pf, u * 4 + (k + 1))
                            for c in range(2):
                                last = nc.tensor.matmul(pp[k][:, 0:wid], oh[:, par, 2 * k + c, :],
                                                        val[:, par, 2 * k + c, 0:wid], start=(c == 0), stop=(c == 1))
                            last.then_inc(s_p, 1)
                        e.wait_ge(s_p, u * 4 + 4)
                        e.sem_inc(s_ohf, 1)
                        if not heads:
                            e.sem_inc(s_free, 1)
                    steps(e, NBODY, step)

                if heads:
                    @blk.scalar
                    def _(e):
                        def step(u, par, i):
                            e.wait_ge(s_ohf, u + 1)
                            nc.scalar.copy(val[:, par, :, D:W8], sc[:, bass.ds(u * BODY, BODY), :]).then_inc(s_ex, 1)
                        steps(e, NBODY, step)

                @blk.vector
                def _(e):
                    L = Link(e, s_v)
                    if heads:
                        e.sem_inc(s_free, 2)
                    e.sem_inc(s_pf, 4)
                    L.step(nc.vector.memset(acc[:, 0:T, :], 0.0))
                    base = 1
                    nstep = (1 if mode == "weight" else 0) + 4 + (4 if heads else 0)

                    def onehot(u, par):
                        e.wait_ge(s_ohf, u + 1)
                        ins = nc.vector.tensor_tensor(oh[:, par, :, :], bc(iota_row[:, :], 1, BODY),
                                                      bc(lo_s[:, bass.ds(u * BODY, BODY)], 2, P), ALU.is_equal)
                        if mode == "weight":
                            ins.then_inc(s_v2, 1)
                            e.wait_ge(s_v2, u + 1)
                            ins = nc.vector.tensor_tensor(oh[:, par, :, :], oh[:, par, :, :],
                                                          bc(w_s[:, bass.ds(u * BODY, BODY)], 2, P), ALU.mult)
                        ins.then_inc(s_oh, 1)

                    onehot(0, 0)

                    def step(u, par, i):
                        tl = tiles_of(mybir.EngineType.DVE, u)
                        if heads:
                            e.wait_ge(s_g[par], i * (16 * BODY) + 16 * BODY)
                            e.wait_ge(s_ohf, u + 1)
                            for k in range(4):
                                hw = D // heads
                                nc.vector.tensor_tensor(
                                    val[:, par, 2 * k:2 * k + 2, 0:D].rearrange("p c (h x) -> p c h x", h=heads),
                                    ring[:, par, 2 * k:2 * k + 2, :].rearrange("p c (h x) -> p c h x", h=heads),
                                    bc(sc[:, bass.ds(u * BODY + 2 * k, 2), 0:heads], 3, hw), ALU.mult).then_inc(s_val, 1)
                        onehot(u + 1, 1 - par)
                        if heads:
                            e.wait_ge(s_val, u * 4 + 4)
                            e.sem_inc(s_free, 1)
                        for k in range(4):
                            e.wait_ge(s_p, u * 4 + (k + 1))
                            e.wait_ge(s_v, u * 4 + (k + 1))
                            a = acc[:, bass.ds(tl[k], 1), 0:wid].rearrange("p a d -> p (a d)")
                            nc.vector.tensor_tensor(a, a, pp[k][:, 0:wid], ALU.add).then_inc(s_v, 1)
                        e.wait_ge(s_v, u * 4 + 5)
                        e.sem_inc(s_pf, 4)
                    steps(e, NBODY, step)

    KT = 5
    assert T % KT == 0

    def node_products(s, srcs, mm, post, nbank, ndone, types=None, masks=None):
        ns = len(srcs)
        xs = s.sb("xs", [P, KT, ns, D])
        xT = s.sb("xT", [P, KT, ns * D]) if masks is None else s.sb("xT", [P, 3, masks, D])
        ptr = [s.ps(f"ptr{k}", [P, 512]) for k in range(3)]
        po = [s.ps(f"po{k}", [P, 512]) for k in range(nbank)]
        s_st, s_tr, s_xt, s_mm, s_fr, s_v, s_idle = (s.sem(n) for n in ("st", "tr", "xt", "mm", "fr", "v", "idle"))

        def tview(k):
            return ptr[k % 3][:, 0:ns * D]

        def tensor(e):
            def transposes(k):
                for a in range(ns):
                    for h in range(2):
                        last = nc.tensor.transpose(tview(k)[:, a * D + h * P:a * D + (h + 1) * P],
                                                   xs[:, k, a, h * P:(h + 1) * P], ident[:, :])
                last.then_inc(s_tr, 1)
            e.wait_ge(s_st, 1)
            transposes(0)
            with e.Fori(0, T // KT) as i:
                for k in range(KT):
                    e.wait_ge(s_st, i * KT + (k + 2))
                    transposes((k + 1) % KT)
                    e.wait_ge(s_xt, i * KT + (k + 1))
                    cnt_ = [0, 0]

                    def wait():
                        cnt_[0] += 1
                        e.wait_ge(s_fr, i * (KT * ndone) + (k * ndone + cnt_[0]))

                    def done(ins):
                        cnt_[1] += 1
                        ins.then_inc(s_mm, 1)
                    mm(e, k, po, xT, wait, done)
                    assert cnt_ == [ndone, ndone]

        def scalar(e, extra=None):
            def stage_in(t, k):
                for a, f in enumerate(srcs):
                    last = nc.scalar.copy(xs[:, k, a, :], f(t))
                last.then_inc(s_st, 1)
            if extra:
                extra(e)
            stage_in(0, 0)
            with e.Fori(0, T // KT) as i:
                for k in range(KT):
                    stage_in(i * KT + (k + 1), (k + 1) % KT)
                    e.wait_ge(s_tr, i * KT + (k + 1))
                    if masks is None:
                        nc.scalar.copy(xT[:, k, :], tview(k)).then_inc(s_xt, 1)

        def vector(e, setup=None, fin=None, per=None):
            L = Link(e, s_v, s_idle)
            if setup:
                setup(e, L)
            e.sem_inc(s_fr, credit)
            with L.loop(T // KT, per * KT) as i:
                for k in range(KT):
                    t = i * KT + k
                    if masks is not None:
                        e.wait_ge(s_tr, i * KT + (k + 1))
                        for m in range(masks):
                            last = nc.vector.scalar_tensor_tensor(
                                xT[:, k % 3, m, :].rearrange("p (h n) -> p h n", h=2),
                                bc(types[:, bass.ds(t * P, P)], 1, 2), float(m),
                                tview(k).rearrange("p (h n) -> p h n", h=2), ALU.is_equal, ALU.mult)
                        last.then_inc(s_xt, 1)

                    def wait(g):
                        e.wait_ge(s_mm, i * (KT * ndone) + (k * ndone + g + 1))

                    def free(n=1):
                        e.sem_inc(s_fr, n)
                    post(e, L, t, k, po, wait, free)
            if fin:
                fin(e, L)
        credit = ndone * nbufs(nbank, ndone)
        return tensor, scalar, vector

    def nbufs(nbank, ndone):
        return KT if nbank == KT else 1

    def layer_norm(dst, mv, g=None, b=None, stats_of=None):
        with stage() as s:
            rstd = s.sb("rstd", [P, T])
            gb = s.sb("gb", [P, 2, D]) if g is not None else None
            s_q, s_a, s_v, s_gb = (s.sem(n) for n in ("q", "a", "v", "gb"))
            with nc.Block() as blk:
                if g is not None:
                    @blk.sync
                    def _(e):
                        e.dma_start(gb[:, 0, :], g.to_broadcast([P, D])).then_inc(s_gb, 16)
                        e.dma_start(gb[:, 1, :], b.to_broadcast([P, D])).then_inc(s_gb, 16)

                @blk.scalar
                def _(e):
                    nc.scalar.activation(rstd[:, :], mv[:, :, 1], ACT.Sqrt, bias=eps_c[:, :]).then_inc(s_a, 1)

                @blk.vector
                def _(e):
                    L = Link(e, s_v)
                    e.wait_ge(s_a, 1)
                    L.step(nc.vector.reciprocal(rstd[:, :], rstd[:, :]))
                    for t in range(T):
                        L.do(nc.vector.tensor_scalar(dst[:, t, :], dst[:, t, :], mv[:, t, 0:1], rstd[:, t:t + 1],
                                                     ALU.subtract, ALU.mult))
                    L.wait()
                    if g is not None:
                        e.wait_ge(s_gb, 32)
                        L.step(nc.vector.tensor_tensor(dst[:, 0:T, :], dst[:, 0:T, :], bc(gb[:, 0, :], 1, T), ALU.mult))
                        L.step(nc.vector.tensor_tensor(dst[:, 0:T, :], dst[:, 0:T, :], bc(gb[:, 1, :], 1, T), ALU.add))

    mv = keep("mv", [P, T, 2])

    def stats(L, st, dst, t):
        L.alone()
        L.step(nc.vector.bn_stats(st[:, 0:6], dst))
        L.alone()
        L.step(nc.vector.bn_aggr(st[:, 6:8], st[:, 0:6]))
        L.do(nc.vector.tensor_copy(tile(mv, t, 2), st[:, 6:8]))

    def tile(a, t, w=D):
        return a[:, bass.ds(t, 1), 0:w].rearrange("p a d -> p (a d)")

    def load_kn(e, dst, w, sem):
        e.dma_start(dst, w.rearrange("(h p) m -> p h m", p=P)).then_inc(sem, 16)

    def gnn0():
        sum_edges(src_i, io["x"], "plain")
        with stage() as s:
            W = s.sb("W", [P, 2, 2, D])
            st = s.sb("st", [P, 8])
            s_w = s.sem("w")

            def mm(e, k, po, xT, wait, done):
                wait()
                for a in range(2):
                    for h in range(2):
                        last = nc.tensor.matmul(po[k][:, 0:D],
                                                xT[:, k, a * D + h * P:a * D + (h + 1) * P], W[:, a, h, :],
                                                start=(a + h == 0), stop=(a + h == 2))
                done(last)

            def post(e, L, t, k, po, wait, free):
                wait(0)
                L.step(nc.vector.scalar_tensor_tensor(tile(X, t), po[k][:, 0:D], 0.0, tile(X, t), ALU.max, ALU.add))
                free()
                stats(L, st, tile(X, t), t)
                L.wait()
            tens, scal, vec = node_products(s, [lambda t: tile(X, t), lambda t: tile(acc, t)], mm, post, KT, 1)
            with nc.Block() as blk:
                @blk.sync
                def _(e):
                    load_kn(e, W[:, 0, :, :], io["L0_gnn_W"], s_w)
                    load_kn(e, W[:, 1, :, :], io["L0_gnn_M"], s_w)

                @blk.tensor
                def _(e):
                    e.wait_ge(s_w, 32)
                    tens(e)

                blk.scalar(scal)
                blk.vector(lambda e: vec(e, per=4))
        layer_norm(X, mv)

    def gat_layer(src, dst, W_in, al, ar, b, last_layer):
        with ExitStack() as es:
            Qs = es.enter_context(nc.sbuf_tensor(nc.make_name("Qs", True), [P, T, 3, HD], BF16))
            with stage() as s:
                W = s.sb("W", [P, 2, W8])
                ab = s.sb("ab", [P, 2, D])
                wp = s.sb("wp", [P, D])
                el = s.sb("el", [P, T, HD])
                er = s.sb("er", [P, T, HD])
                s_w, s_z, s_o, s_ww = s.sem("w"), s.sem("z"), s.sem("o"), s.sem("ww")

                def mm(e, k, po, xT, wait, done):
                    wait()
                    for h in range(2):
                        last = nc.tensor.matmul(po[k][:, 0:W8], xT[:, k, h * P:(h + 1) * P], W[:, h, :],
                                                start=(h == 0), stop=(h == 1))
                    done(last)

                def post(e, L, t, k, po, wait, free):
                    wait(0)
                    L.step(nc.vector.tensor_copy(tile(acc, t, W8), po[k][:, 0:W8]))
                    free()

                def setup(e, L):
                    e.wait_ge(s_w, 48)
                    for h in range(2):
                        for j in range(2):
                            L.step(nc.vector.tensor_tensor(wp[:, :], W[:, h, 0:D], ab[:, j, :], ALU.mult))
                            L.step(nc.vector.tensor_reduce(W[:, h, D + 4 * j:D + 4 * j + 4],
                                                           wp[:, :].rearrange("p (h x) -> p h x", h=4), AX.X, ALU.add))
                    e.sem_inc(s_ww, 1)

                def fin(e, L):
                    for o, a in ((el, 0), (er, 4)):
                        L.do(nc.vector.tensor_copy(o[:, :, :].rearrange("p t (r h) -> p t r h", r=2),
                                                   bc(acc[:, 0:T, D + a:D + a + 4], 2, 2)))
                    L.wait()
                    e.sem_inc(s_z, 1)
                    split3(L, Qs, er)
                tens, scal, vec = node_products(s, [lambda t: tile(src, t)], mm, post, KT, 1)
                with nc.Block() as blk:
                    @blk.sync
                    def _(e):
                        load_kn(e, W[:, :, 0:D], W_in, s_w)
                        for j, a in enumerate((al, ar)):
                            e.dma_start(ab[:, j, :], a.rearrange("h d -> (h d)").unsqueeze(0).to_broadcast([P, D])
                                        ).then_inc(s_w, 16)
                        e.wait_ge(s_z, 1)
                        e.dma_start(tab_z.rearrange("(t p) d -> p t d", p=P), acc[:, 0:T, 0:D]).then_inc(s_o, 16)
                        e.dma_start(tab_e.rearrange("(t p) d -> p t d", p=P), el[:, :, :]).then_inc(s_o, 16)
                        e.wait_ge(s_o, 32)

                    @blk.tensor
                    def _(e):
                        e.wait_ge(s_ww, 1)
                        tens(e)

                    blk.scalar(scal)
                    blk.vector(lambda e: vec(e, setup=setup, fin=fin, per=1))
            score_edges(Qs, HD, src_i, tab_e, True)
        softmax()
        sum_edges(src_i, tab_z, 4)
        with stage() as s:
            r = s.sb("r", [P, T, HD])
            Y = s.sb("Y", [P, KT, D])
            Z = s.sb("Z", [P, KT, D])
            bb = s.sb("bb", [P, D])
            st = s.sb("st", [P, 8])
            s_b, s_v, s_m, s_a, s_idle = (s.sem(n) for n in ("b", "v", "m", "a", "idle"))
            with nc.Block() as blk:
                @blk.sync
                def _(e):
                    e.dma_start(bb[:, :], b.unsqueeze(0).to_broadcast([P, D])).then_inc(s_b, 16)

                @blk.scalar
                def _(e):
                    with e.Fori(0, T // KT) as i:
                        e.wait_ge(s_m, i + 1)
                        nc.scalar.activation(Z[:, :, :], Z[:, :, :], ACT.Exp).then_inc(s_a, 1)

                @blk.vector
                def _(e):
                    L = Link(e, s_v, s_idle)
                    L.step(nc.vector.tensor_scalar(r[:, :, :], acc[:, 0:T, D:W8], 0.5, None, ALU.max))
                    L.step(nc.vector.reciprocal(r[:, :, :], r[:, :, :]))
                    e.wait_ge(s_b, 16)
                    with L.loop(T // KT, 7 + 3 * KT if last_layer else 6) as i:
                        tk = lambda a, w=D: a[:, bass.ds(i * KT, KT), 0:w]
                        L.step(nc.vector.tensor_tensor(Y[:, :, :].rearrange("p t (h x) -> p t h x", h=4),
                                                       tk(acc).rearrange("p t (h x) -> p t h x", h=4),
                                                       bc(tk(r, 4), 3, D // 4), ALU.mult))
                        L.step(nc.vector.tensor_tensor(Y[:, :, :], Y[:, :, :], tk(src), ALU.add))
                        L.step(nc.vector.tensor_tensor(Y[:, :, :], Y[:, :, :], bc(bb[:, :], 1, KT), ALU.add))
                        L.do(nc.vector.tensor_scalar(Z[:, :, :], Y[:, :, :], 0.0, None, ALU.min))
                        L.wait()
                        e.sem_inc(s_m, 1)
                        e.wait_ge(s_a, i + 1)
                        L.step(nc.vector.tensor_scalar(Z[:, :, :], Z[:, :, :], -1.0, None, ALU.add))
                        if last_layer:
                            L.step(nc.vector.scalar_tensor_tensor(Y[:, :, :], Y[:, :, :], 0.0, Z[:, :, :], ALU.max, ALU.add))
                            L.step(nc.vector.tensor_tensor(tk(dst), tk(dst), Y[:, :, :], ALU.add))
                            for k in range(KT):
                                stats(L, st, tile(dst, i * KT + k), i * KT + k)
                                L.wait()
                        else:
                            L.step(nc.vector.scalar_tensor_tensor(tk(dst), Y[:, :, :], 0.0, Z[:, :, :], ALU.max, ALU.add))

    def split3(L, Qs, q):
        for r in range(3):
            L.step(nc.vector.tensor_copy(Qs[:, :, r, :], q[:, :, :]))
            if r < 2:
                L.step(nc.vector.tensor_tensor(q[:, :, :], q[:, :, :], Qs[:, :, r, :], ALU.subtract))

    def gnn1():
        gat_layer(X, H, io["L1_gnn_W0"], io["L1_gnn_al0"], io["L1_gnn_ar0"], io["L1_gnn_b0"], False)
        gat_layer(H, X, io["L1_gnn_W1"], io["L1_gnn_al1"], io["L1_gnn_ar1"], io["L1_gnn_b1"], True)
        layer_norm(X, mv)

    NT, NE, HW = 4, 3, D // HD
    KW = (2 + NE) * P
    HALFS = range(2)

    def gnn2_tables(l, Qs):
        with ExitStack() as es:
            W = es.enter_context(nc.sbuf_tensor(nc.make_name("Wt", True), [P, 2, NT, KW], F32))
            with stage() as s:
                WK = s.sb("WK", [P, 2 * NT, P])
                WKT = s.sb("WKT", [P, 2 * NT, P])
                WE = s.sb("WE", [P, 2, NE, P])
                mus = s.sb("mus", [P, 2, NE])
                pk = [s.ps(f"pk{k}", [P, 512]) for k in range(2)]
                pm = [s.ps(f"pm{k}", [P, 512]) for k in range(4)]
                s_z, s_w, s_t, s_e, s_m, s_v, s_mf = (s.sem(n) for n in ("z", "w", "t", "e", "m", "v", "mf"))
                with nc.Block() as blk:
                    @blk.sync
                    def _(e):
                        e.wait_ge(s_z, 3)
                        n = 0
                        for q in range(4):
                            rows = slice(q * HW, (q + 1) * HW)
                            for h in HALFS:
                                hd = 4 * h + q
                                for name, o in (("W_Q", W[rows, h, :, q * HW:(q + 1) * HW]),
                                                ("W_V", W[rows, h, :, KW - P + q * HW:KW - P + (q + 1) * HW]),
                                                ("W_K", WK[rows, h * NT:(h + 1) * NT, q * HW:(q + 1) * HW]),
                                                ("W_E", WE[rows, h, :, q * HW:(q + 1) * HW])):
                                    a = io["L2_gnn_" + name][bass.ds(l, 1), :, hd, :, :].rearrange("o t d x -> d (o t) x")
                                    e.dma_start(o, a).then_inc(s_w, 16)
                                    n += 1
                                e.dma_start(mus[rows, h, :], io["L2_gnn_mu"][bass.ds(l, 1), hd, :].to_broadcast([HW, NE])
                                            ).then_inc(s_w, 16)
                                n += 1
                        e.wait_ge(s_w, 16 * n)

                    @blk.gpsimd
                    def _(e):
                        nc.gpsimd.memset(W[:, :, :, :], 0.0).then_inc(s_z, 1)

                    @blk.tensor
                    def _(e):
                        e.wait_ge(s_w, 16 * 40)
                        for j in range(2 * NT):
                            last = nc.tensor.transpose(pk[j // 4][:, (j % 4) * P:(j % 4 + 1) * P], WK[:, j, :], ident[:, :])
                            if j % 4 == 3:
                                last.then_inc(s_t, 1)
                        e.wait_ge(s_e, 2)
                        for j in range(2 * NT):
                            if j >= 4:
                                e.wait_ge(s_mf, j - 3)
                            nc.tensor.matmul(pm[j % 4][:, 0:NE * P], WKT[:, j, :],
                                             WE[:, j // NT, :, :].rearrange("p t x -> p (t x)"), start=True, stop=True
                                             ).then_inc(s_m, 1)

                    @blk.scalar
                    def _(e):
                        for k in range(2):
                            e.wait_ge(s_t, k + 1)
                            nc.scalar.copy(WKT[:, 4 * k:4 * k + 4, :].rearrange("p j x -> p (j x)"), pk[k][:, :]).then_inc(s_e, 1)

                    @blk.vector
                    def _(e):
                        L = Link(e, s_v)
                        nc.vector.memset(WK[:, :, :], 0.0).then_inc(s_z, 1)
                        nc.vector.memset(WE[:, :, :, :], 0.0).then_inc(s_z, 1)
                        e.wait_ge(s_w, 16 * 40)
                        L.step(nc.vector.tensor_scalar(mus[:, :, :], mus[:, :, :], float(HW) ** -0.5, None, ALU.mult))
                        for j in range(2 * NT):
                            h, t = divmod(j, NT)
                            e.wait_ge(s_m, j + 1)
                            nc.vector.tensor_tensor(W[:, h, t, P:P + NE * P].rearrange("p (t x) -> p t x", t=NE),
                                                    pm[j % 4][:, 0:NE * P].rearrange("p (t x) -> p t x", t=NE),
                                                    bc(mus[:, h, :], 2, P), ALU.mult).then_inc(s_mf, 1)
                        e.wait_ge(s_mf, 2 * NT)
            with stage() as s:
                types = sc[:, :, :].rearrange("p c h -> p (c h)").bitcast(I32)[:, 0:NP]
                kv = acc[:, :, :].rearrange("p t d -> p (t d)")[:, 0:KT * 2 * KW].rearrange("p (k h c) -> p k h c", k=KT, h=2)
                q2 = s.sb("q2", [P, 2, D])
                s_ty, s_tz, s_kv, s_ko = s.sem("ty"), s.sem("tz"), s.sem("kv"), s.sem("ko")
                s_o = [s.sem(f"o{k}") for k in range(KT)]

                def mm(e, k, po, xT, wait, done):
                    for h in HALFS:
                        wait()
                        for t in range(NT):
                            last = nc.tensor.matmul(po[h][:, :], xT[:, k % 3, t, h * P:(h + 1) * P], W[:, h, t, 0:KW - P],
                                                    start=(t == 0), stop=(t == NT - 1))
                        done(last)
                    wait()
                    for h in HALFS:
                        for t in range(NT):
                            last = nc.tensor.matmul(po[2][:, h * P:(h + 1) * P], xT[:, k % 3, t, h * P:(h + 1) * P],
                                                    W[:, h, t, KW - P:KW], start=(t == 0), stop=(t == NT - 1))
                    done(last)

                def post(e, L, t, k, po, wait, free):
                    e.wait_ge(s_ko, t + 1)
                    for h in HALFS:
                        wait(h)
                        L.step(nc.vector.tensor_copy(kv[:, k, h, 0:KW - P], po[h][:, :]))
                        free()
                    wait(2)
                    L.step(nc.vector.tensor_copy(kv[:, k, :, KW - P:KW], po[2][:, 0:D].rearrange("p (h x) -> p h x", h=2)))
                    free()
                    e.sem_inc(s_kv, 1)
                    Qt = Qs[:, bass.ds(t, 1), :, :].rearrange("p a r d -> p (a r) d")
                    hv = lambda a: a.rearrange("p (h x) -> p h x", h=2)
                    q = kv[:, k, :, 0:P]
                    L.step(nc.vector.tensor_copy(hv(Qt[:, 0, :]), q))
                    L.step(nc.vector.tensor_tensor(hv(q2[:, 0, :]), q, hv(Qt[:, 0, :]), ALU.subtract))
                    L.step(nc.vector.tensor_copy(Qt[:, 1, :], q2[:, 0, :]))
                    L.step(nc.vector.tensor_tensor(Qt[:, 2, :], q2[:, 0, :], Qt[:, 1, :], ALU.subtract))

                def setup(e, L):
                    e.wait_ge(s_ty, 16)
                tens, scal, vec = node_products(s, [lambda t: tile(H, t)], mm, post, 3, 3, types=types, masks=NT)
                with nc.Block() as blk:
                    @blk.gpsimd
                    def _(e):
                        nc.gpsimd.memset(types[:, N:], 0).then_inc(s_tz, 1)

                    @blk.sync
                    def _(e):
                        e.dma_start(types[:, 0:N], io["node_type_4"].unsqueeze(0).to_broadcast([P, N])).then_inc(s_ty, 16)
                        e.sem_inc(s_ko, KT)
                        k_v = tab_k.rearrange("(s t p) (h x) -> p h s t x", s=NE, p=P, h=2)
                        v_v = tab_v.rearrange("(t p) (h x) -> p h t x", p=P, h=2)
                        with e.Fori(0, T // KT) as i:
                            for k in range(KT):
                                e.wait_ge(s_kv, i * KT + (k + 1))
                                for h in HALFS:
                                    e.dma_start(k_v[:, h, :, bass.ds(i * KT + k, 1), :].rearrange("p s t x -> p s (t x)"),
                                                kv[:, k, h, P:KW - P].rearrange("p (s x) -> p s x", s=NE)).then_inc(s_o[k], 16)
                                e.dma_start(v_v[:, :, bass.ds(i * KT + k, 1), :].rearrange("p h t x -> p h (t x)"),
                                            kv[:, k, :, KW - P:KW]).then_inc(s_o[k], 16)
                            for k in range(KT):
                                e.wait_ge(s_o[k], i * 48 + 48)
                                e.sem_inc(s_ko, 1)

                    @blk.tensor
                    def _(e):
                        tens(e)

                    @blk.scalar
                    def _(e):
                        scal(e)

                    @blk.vector
                    def _(e):
                        e.wait_ge(s_tz, 1)
                        vec(e, setup=setup, per=7)

    def gnn2_layer(l):
        row = lambda name: io["L2_gnn_" + name][bass.ds(l, 1), :]
        with ExitStack() as es:
            Qs = es.enter_context(nc.sbuf_tensor(nc.make_name("Qs", True), [P, T, 3, D], BF16))
            gnn2_tables(l, Qs)
            score_edges(Qs, D, idx3_i, tab_k, False)
        softmax()
        sum_edges(src_i, tab_v, HD)
        with stage() as s:
            W = s.sb("W", [P, 2, D])
            r = s.sb("r", [P, T, HD])
            bo = s.sb("bo", [P, D])
            st = s.sb("st", [P, 8])
            s_w, s_b, s_n = s.sem("w"), s.sem("b"), s.sem("n")

            def mm(e, k, po, xT, wait, done):
                wait()
                for h in HALFS:
                    last = nc.tensor.matmul(po[k][:, 0:D], xT[:, k, h * P:(h + 1) * P], W[:, h, :],
                                            start=(h == 0), stop=(h == 1))
                done(last)

            def setup(e, L):
                L.step(nc.vector.tensor_scalar(r[:, :, :], acc[:, 0:T, D:W8], 1e-10, None, ALU.add))
                L.step(nc.vector.reciprocal(r[:, :, :], r[:, :, :]))
                av = acc[:, 0:T, 0:D].rearrange("p t (h x) -> p t h x", h=HD)
                L.step(nc.vector.tensor_tensor(av, av, bc(r[:, :, :], 3, HW), ALU.mult))
                e.sem_inc(s_n, 1)
                e.wait_ge(s_b, 16)
                L.step(nc.vector.tensor_tensor(H[:, 0:T, :], H[:, 0:T, :], bc(bo[:, :], 1, T), ALU.add))

            def post(e, L, t, k, po, wait, free):
                wait(0)
                L.step(nc.vector.scalar_tensor_tensor(tile(H, t), po[k][:, 0:D], 1.0, tile(H, t), ALU.mult, ALU.add))
                free()
                stats(L, st, tile(H, t), t)
                L.wait()
            tens, scal, vec = node_products(s, [lambda t: tile(acc, t)], mm, post, KT, 1)
            with nc.Block() as blk:
                @blk.sync
                def _(e):
                    e.dma_start(W[:, :, :], io["L2_gnn_Wo"][bass.ds(l, 1), :, :].rearrange("o (h p) m -> p (o h) m", p=P)
                                ).then_inc(s_w, 16)
                    e.dma_start(bo[:, :], row("bo").to_broadcast([P, D])).then_inc(s_b, 16)

                @blk.tensor
                def _(e):
                    e.wait_ge(s_w, 16)
                    tens(e)

                @blk.scalar
                def _(e):
                    scal(e, extra=lambda e: e.wait_ge(s_n, 1))

                blk.vector(lambda e: vec(e, setup=setup, per=4))
        layer_norm(H, mv, row("ln1_g"), row("ln1_b"))
        FB = 4 * D // P
        with stage() as s:
            w1 = s.sb("w1", [P, 2, 4 * D])
            w2 = s.sb("w2", [P, FB, D])
            b1 = s.sb("b1", [P, FB])
            b2 = s.sb("b2", [P, D])
            xs = s.sb("xs", [P, KT, D])
            xT = s.sb("xT", [P, KT, D])
            hT = s.sb("hT", [P, 2, 4, P])
            st = s.sb("st", [P, 8])
            ptr = [s.ps(f"ptr{k}", [P, 512]) for k in range(3)]
            ph = [s.ps(f"ph{k}", [P, 512]) for k in range(2)]
            po = [s.ps(f"po{k}", [P, 512]) for k in range(3)]
            s_w, s_st, s_tr, s_xt, s_h, s_g, s_o, s_fr, s_v, s_idle = (
                s.sem(n) for n in ("w", "st", "tr", "xt", "h", "g", "o", "fr", "v", "idle"))
            with nc.Block() as blk:
                @blk.sync
                def _(e):
                    e.dma_start(w1[:, :, :], io["L2_gnn_w1"][bass.ds(l, 1), :, :].rearrange("o (h p) m -> p (o h) m", p=P)
                                ).then_inc(s_w, 16)
                    e.dma_start(w2[:, :, :], io["L2_gnn_w2"][bass.ds(l, 1), :, :].rearrange("o (f p) m -> p (o f) m", p=P)
                                ).then_inc(s_w, 16)
                    with nc.allow_non_contiguous_dma(reason="1024 words"):
                        e.dma_start(b1[:, :], row("b1").rearrange("o (f p) -> p (o f)", p=P)).then_inc(s_w, 16)
                    e.dma_start(b2[:, :], row("b2").to_broadcast([P, D])).then_inc(s_w, 16)

                @blk.tensor
                def _(e):
                    def transposes(k):
                        for h in HALFS:
                            last = nc.tensor.transpose(ptr[k % 3][:, h * P:(h + 1) * P], xs[:, k, h * P:(h + 1) * P], ident[:, :])
                        last.then_inc(s_tr, 1)
                    e.wait_ge(s_w, 64)
                    e.wait_ge(s_st, 1)
                    transposes(0)
                    with e.Fori(0, T // KT) as i:
                        for k in range(KT):
                            e.wait_ge(s_st, i * KT + (k + 2))
                            transposes((k + 1) % KT)
                            e.wait_ge(s_xt, i * KT + (k + 1))
                            for g in range(2):
                                for f in range(4):
                                    for h in HALFS:
                                        fb = 4 * g + f
                                        last = nc.tensor.matmul(ph[g][:, f * P:(f + 1) * P], w1[:, h, fb * P:(fb + 1) * P],
                                                                xT[:, k, h * P:(h + 1) * P], start=(h == 0), stop=(h == 1))
                                last.then_inc(s_h, 1)
                            e.wait_ge(s_fr, i * KT + (k + 1))
                            for g in range(2):
                                e.wait_ge(s_g, i * (2 * KT) + (2 * k + g + 1))
                                for f in range(4):
                                    last = nc.tensor.matmul(po[k % 3][:, 0:D], hT[:, g, f, :], w2[:, 4 * g + f, :],
                                                            start=(g + f == 0), stop=(g + f == 4))
                            last.then_inc(s_o, 1)

                @blk.scalar
                def _(e):
                    def stage_in(t, k):
                        nc.scalar.copy(xs[:, k, :], tile(H, t)).then_inc(s_st, 1)
                    e.wait_ge(s_w, 64)
                    stage_in(0, 0)
                    with e.Fori(0, T // KT) as i:
                        for k in range(KT):
                            stage_in(i * KT + (k + 1), (k + 1) % KT)
                            e.wait_ge(s_tr, i * KT + (k + 1))
                            nc.scalar.copy(xT[:, k, :], ptr[k % 3][:, 0:D]).then_inc(s_xt, 1)
                            for g in range(2):
                                e.wait_ge(s_h, i * (2 * KT) + (2 * k + g + 1))
                                for f in range(4):
                                    last = nc.scalar.activation(hT[:, g, f, :], ph[g][:, f * P:(f + 1) * P], ACT.Gelu,
                                                                bias=b1[:, 4 * g + f:4 * g + f + 1])
                                last.then_inc(s_g, 1)

                @blk.vector
                def _(e):
                    L = Link(e, s_v, s_idle)
                    e.wait_ge(s_w, 64)
                    e.sem_inc(s_fr, 2)
                    with L.loop(T // KT, 5 * KT) as i:
                        for k in range(KT):
                            t = i * KT + k
                            e.wait_ge(s_o, t + 1)
                            L.step(nc.vector.scalar_tensor_tensor(tile(H, t), po[k % 3][:, 0:D], 1.0, tile(H, t),
                                                                  ALU.mult, ALU.add))
                            e.sem_inc(s_fr, 1)
                            L.step(nc.vector.tensor_tensor(tile(H, t), tile(H, t), b2[:, :], ALU.add))
                            stats(L, st, tile(H, t), t)
                            L.wait()
        layer_norm(H, mv, row("ln2_g"), row("ln2_b"))

    def gnn2():
        copy_tiles(H, X)
        with nc.Fori(0, 3) as l:
            gnn2_layer(l)
        tile_stats(H)
        layer_norm(H, mv, io["L2_gnn_out_g"].unsqueeze(0), io["L2_gnn_out_b"].unsqueeze(0))
        add_stats(X, lambda t: tile(H, t))
        layer_norm(X, mv)

    def copy_tiles(dst, src):
        with stage() as s:
            with nc.Block() as blk:
                @blk.vector
                def _(e):
                    nc.vector.tensor_copy(dst[:, 0:T, :], src[:, 0:T, :])

    def tile_stats(a):
        add_stats(a, None)

    def add_stats(a, b):
        with stage() as s:
            st = s.sb("st", [P, 8])
            s_v, s_idle = s.sem("v"), s.sem("idle")
            with nc.Block() as blk:
                @blk.vector
                def _(e):
                    L = Link(e, s_v, s_idle)
                    with L.loop(T // KT, KT * (4 if b else 3)) as i:
                        for k in range(KT):
                            t = i * KT + k
                            if b:
                                L.step(nc.vector.tensor_tensor(tile(a, t), tile(a, t), b(t), ALU.add))
                            stats(L, st, tile(a, t), t)
                            L.wait()

    def gnn3():
        NR = 8
        with stage() as s:
            W = s.sb("W", [P, 2, NR, P])
            hs = acc[:, :, :].rearrange("p t d -> p (t d)")[:, 0:2 * NR * D].rearrange("p (k h c) -> p k h c", k=2, h=2)
            s_z, s_w, s_c, s_ho = s.sem("z"), s.sem("w"), s.sem("c"), s.sem("ho")
            s_o = s.sem("o")

            def mm(e, k, po, xT, wait, done):
                for h in HALFS:
                    wait()
                    for j in range(2):
                        last = nc.tensor.matmul(po[2 * h + j][:, :], xT[:, k, h * P:(h + 1) * P],
                                                W[:, h, 4 * j:4 * j + 4, :].rearrange("p r x -> p (r x)"), start=True, stop=True)
                    done(last)

            def post(e, L, t, k, po, wait, free):
                e.wait_ge(s_ho, t + 1)
                for h in HALFS:
                    wait(h)
                    for j in range(2):
                        L.do(nc.vector.tensor_copy(hs[:, 0, h, j * 512:(j + 1) * 512], po[2 * h + j][:, :]))
                    L.wait()
                    free()
                e.sem_inc(s_c, 1)
            tens, scal, vec = node_products(s, [lambda t: tile(X, t)], mm, post, 4, 2)
            with nc.Block() as blk:
                @blk.sync
                def _(e):
                    e.wait_ge(s_z, 1)
                    for q in range(4):
                        for h in HALFS:
                            a = io["L3_gnn_weight"].rearrange("r (b i o) -> b i r o", b=HD, i=HW)[4 * h + q]
                            e.dma_start(W[q * HW:(q + 1) * HW, h, :, q * HW:(q + 1) * HW], a).then_inc(s_w, 16)
                    e.sem_inc(s_ho, 1)
                    h_v = tab_h.rearrange("(r t p) (h x) -> p h r t x", r=NR, p=P, h=2)
                    with e.Fori(0, T) as i:
                        e.wait_ge(s_c, i + 1)
                        for h in HALFS:
                            e.dma_start(h_v[:, h, :, bass.ds(i, 1), :].rearrange("p r t x -> p r (t x)"),
                                        hs[:, 0, h, :].rearrange("p (r x) -> p r x", r=NR)).then_inc(s_o, 16)
                        e.wait_ge(s_o, i * 32 + 32)
                        e.sem_inc(s_ho, 1)

                @blk.gpsimd
                def _(e):
                    nc.gpsimd.memset(W[:, :, :, :], 0.0).then_inc(s_z, 1)

                @blk.tensor
                def _(e):
                    e.wait_ge(s_w, 128)
                    tens(e)

                blk.scalar(scal)
                blk.vector(lambda e: vec(e, per=4))
        sum_edges(idx8_i, tab_h, "weight")
        add_stats(X, lambda t: tile(acc, t))
        layer_norm(X, mv)
        with stage() as s:
            s_o = s.sem("o")
            with nc.Block() as blk:
                @blk.sync
                def _(e):
                    e.dma_start(out[0:(T - 1) * P, :].rearrange("(t p) d -> p t d", p=P), X[:, 0:T - 1, :]).then_inc(s_o, 16)
                    e.dma_start(out[(T - 1) * P:N, :], X[0:TAIL, T - 1, :]).then_inc(s_o, 16)
                    e.wait_ge(s_o, 32)

    gnn0()
    gnn1()
    gnn2()
    gnn3()

    outer.close()


_INS = ["x", "src", "dst", "edge_type_3", "edge_type_8", "edge_weight", "node_type_4", "L0_gnn_W", "L0_gnn_M",
        "L1_gnn_W0", "L1_gnn_al0", "L1_gnn_ar0", "L1_gnn_b0", "L1_gnn_W1", "L1_gnn_al1", "L1_gnn_ar1", "L1_gnn_b1",
        "L2_gnn_W_Q", "L2_gnn_W_K", "L2_gnn_W_V", "L2_gnn_W_E", "L2_gnn_mu", "L2_gnn_Wo", "L2_gnn_bo",
        "L2_gnn_ln1_g", "L2_gnn_ln1_b", "L2_gnn_ln2_g", "L2_gnn_ln2_b", "L2_gnn_w1", "L2_gnn_b1", "L2_gnn_w2",
        "L2_gnn_b2", "L2_gnn_out_g", "L2_gnn_out_b", "L3_gnn_weight"]


def kernel(**inputs):
    import concourse.bacc as _bacc
    from concourse.bass_utils import run_bass_kernel_spmd as _run

    nc = _bacc.Bacc("TRN2", target_bir_lowering=False, num_devices=1)
    arrays, io = {}, {}
    for name in _INS:
        a = np.ascontiguousarray(inputs[name])
        arrays[f"in_{name}"] = a
        io[name] = nc.dram_tensor(f"in_{name}", a.shape, mybir.dt.from_np(a.dtype), kind="ExternalInput").ap()
    io["out"] = nc.dram_tensor("out_0", (N, D), F32, kind="ExternalOutput").ap()
    build(nc, io)
    r = _run(nc, [arrays], core_ids=[0])
    return r.results[0]["out_0"]
```

```python
from contextlib import ExitStack, contextmanager

import numpy as np

import concourse.bass as bass
from concourse import mybir

F32 = mybir.dt.float32
BF16 = mybir.dt.bfloat16
I32 = mybir.dt.int32
ALU = mybir.AluOpType
ACT = mybir.ActivationFunctionType
AX = mybir.AxisListType

P = 128
N = 3125
D = 256
E = 53125
T = -(-N // P)
NP = T * P
TAIL = N - (T - 1) * P
HD = 8

EP, EJ = 125, 425
RG, RP = 5, 85
SORT_J = 17
NSORT = EJ // SORT_J

PAIRS = (E + 255 * T) // 256
PAIRS += -PAIRS % 8
CH = 2 * PAIRS
BODY = 8
NBODY = CH // BODY
HALF = NBODY // 2
WC = P // HD
NW = CH // WC
REC = 8
F_SRC, F_I3, F_I8, F_W, F_LO, F_DST = range(6)
LG, LP = 4, CH // 4
BIG = 1e30
EPS = 1e-5
W8 = D + HD
assert CH % WC == 0 and NW % 2 == 1 and NBODY % 2 == 0 and CH % LG == 0 and EP * EJ == E and CH <= 512
assert EJ == RG * RP and EJ % SORT_J == 0


class Link:

    def __init__(self, eng, sem, idle=None):
        self.idle = idle
        self.eng, self.sem, self.base, self.n, self.i, self.per = eng, sem, 0, 0, None, 0

    def do(self, ins):
        ins.then_inc(self.sem, 1)
        self.n += 1
        return self.n

    def wait(self, at=None):
        v = self.base + (self.n if at is None else at)
        self.eng.wait_ge(self.sem, v if self.i is None else self.i * self.per + v)

    def step(self, ins):
        self.do(ins)
        self.wait()

    def alone(self):
        self.eng.sem_inc(self.idle, 1)

    @contextmanager
    def loop(self, count, per):
        self.base, self.n = self.base + self.n, 0
        with self.eng.Fori(0, count) as i:
            self.i, self.per = i, per
            yield i
            assert self.n == per, (self.n, per)
        self.i, self.n = None, 0
        self.base += count * per


def build(nc, io):
    out = io["out"]
    rec = nc.dram_tensor("rec", (CH * P, REC), F32, kind="Internal").ap()
    tab_z = nc.dram_tensor("tab_z", (NP, W8), F32, kind="Internal").ap()
    tab_kv = nc.dram_tensor("tab_kv", (3 * NP, 2 * D), F32, kind="Internal").ap()
    keep_x = nc.dram_tensor("keep_x", (P, T * D), F32, kind="Internal").ap()
    keep_i8 = nc.dram_tensor("keep_i8", (P, CH), I32, kind="Internal").ap()
    keep_w = nc.dram_tensor("keep_w", (P, CH), F32, kind="Internal").ap()
    tab_h = nc.dram_tensor("tab_h", (8 * NP, D), F32, kind="Internal").ap()

    outer = ExitStack()

    def keep(name, shape, dt=F32):
        return outer.enter_context(nc.sbuf_tensor(name, shape, dt))

    iota_row = keep("iota_row", [P, P])
    ident = keep("ident", [P, P])
    ident_b = keep("ident_b", [P, P], BF16)
    eps_c = keep("eps_c", [P, 1])
    X = keep("X", [P, T + 1, D])
    src_i = keep("src_i", [P, CH], I32)
    idx3_i = keep("idx3_i", [P, CH], I32)
    lo_s = keep("lo_s", [P, CH + BODY])
    tile_q = keep("tile_q", [1, PAIRS + 2], I32)

    @contextmanager
    def stage():
        with nc.cleanup_on_exit():
            with ExitStack() as st:
                class S:
                    def sb(self, name, shape, dt=F32):
                        return st.enter_context(nc.sbuf_tensor(nc.make_name(name, True), shape, dt))

                    def ps(self, name, shape, dt=F32):
                        return st.enter_context(nc.psum_tensor(nc.make_name(name, True), shape, dt))

                    def sem(self, name):
                        return nc.alloc_semaphore(nc.make_name(name, True))
                yield S()
        nc.all_engine_barrier()

    def steps(e, n, fn):
        with e.Fori(0, n // 2) as i:
            fn(i * 2, 0, i)
            fn(i * 2 + 1, 1, i)
        if n % 2:
            fn(n - 1, 0, n // 2)

    def bc(ap, axis, n):
        v = ap.unsqueeze(axis)
        shape = list(v.shape)
        shape[axis] = n
        return v.to_broadcast(shape)

    with stage() as s:
        s_x, s_c, s_z, s_i = s.sem("x"), s.sem("c"), s.sem("z"), s.sem("i")
        io_i = s.sb("io_i", [P, P], I32)
        with nc.Block() as blk:
            @blk.gpsimd
            def _(e):
                nc.gpsimd.iota(io_i[:, :], pattern=[[1, P]], base=0, channel_multiplier=0).then_inc(s_i, 1)
                nc.gpsimd.memset(ident[:, :], 0.0).then_inc(s_z, 1)
                e.wait_ge(s_z, 1)
                nc.gpsimd.affine_select(out=ident[:, :], in_=ident[:, :], compare_op=ALU.not_equal, fill=1.0,
                                        base=0, pattern=[[-1, P]], channel_multiplier=1).then_inc(s_c, 1)

            @blk.vector
            def _(e):
                nc.vector.memset(eps_c[:, :], EPS)
                nc.vector.memset(tile_q[:, PAIRS:], 0)
                nc.vector.memset(lo_s[:, CH:], -1.0)
                nc.vector.memset(X[:, T - 1:, :], 0.0).then_inc(s_x, 1)
                e.wait_ge(s_i, 1)
                nc.vector.tensor_copy(iota_row[:, :], io_i[:, :])
                e.wait_ge(s_c, 1)
                nc.vector.tensor_copy(ident_b[:, :], ident[:, :])

            @blk.sync
            def _(e):
                s_d = s.sem("d")
                e.dma_start(X[:, 0:T - 1, :], io["x"][0:(T - 1) * P, :].rearrange("(t p) d -> p t d", p=P)
                            ).then_inc(s_d, 16)
                e.wait_ge(s_x, 1)
                e.dma_start(X[0:TAIL, T - 1, :], io["x"][(T - 1) * P:N, :]).then_inc(s_d, 16)
                e.wait_ge(s_d, 32)

    with ExitStack() as sorting:
        def skeep(name, shape, dt=F32):
            return sorting.enter_context(nc.sbuf_tensor(name, shape, dt))
        R = skeep("R", [EP, EJ, REC])
        hi_c = skeep("hi_c", [EP, EJ])
        oh_hi = skeep("oh_hi", [EP, EJ, T], BF16)
        pa = skeep("pa", [P, EJ, T], BF16)
        pb = skeep("pb", [P, EJ, T], BF16)
        counting = ExitStack()
        cnt = counting.enter_context(nc.sbuf_tensor("cnt", [P, T, EJ], F32))

        with stage() as s:
            rows_i = s.sb("rows_i", [RP, 4, RG * EP], I32)
            rows = s.sb("rows", [RP, 7, RG * EP])
            tmp_i = s.sb("tmp_i", [RP, 2, RG * EP], I32)
            pad = s.sb("pad", [P, CH * REC])
            ptr = [s.ps(f"ptr{k}", [EP, 512]) for k in range(7)]
            s_in, s_p, s_r, s_v, s_t, s_pad = (s.sem(n) for n in ("in", "p", "r", "v", "t", "pad"))
            with nc.Block() as blk:
                @blk.sync
                def _(e):
                    for k, name in enumerate(("src", "dst", "edge_type_3", "edge_type_8")):
                        e.dma_start(rows_i[:, k, :].rearrange("p (g e) -> p g e", g=RG),
                                    io[name].rearrange("(g p e) -> p g e", g=RG, p=RP)).then_inc(s_in, 16)
                    e.dma_start(rows[:, F_W, :].rearrange("p (g e) -> p g e", g=RG),
                                io["edge_weight"].rearrange("(g p e) -> p g e", g=RG, p=RP)).then_inc(s_in, 16)
                    e.wait_ge(s_p, 2)
                    e.dma_start(rec.rearrange("(p c) f -> p (c f)", p=P), pad[:, :]).then_inc(s_pad, 16)
                    e.wait_ge(s_pad, 16)

                @blk.vector
                def _(e):
                    L = Link(e, s_v)
                    nc.vector.memset(pad[:, :], 0.0).then_inc(s_p, 1)
                    e.wait_ge(s_p, 1)
                    nc.vector.memset(pad[:, :].rearrange("p (c f) -> p c f", f=REC)[:, :, F_LO:F_DST + 1], -1.0
                                     ).then_inc(s_p, 1)
                    L.do(nc.vector.memset(R[:, :, F_DST + 1:REC], 0.0))
                    e.wait_ge(s_in, 80)
                    L.do(nc.vector.tensor_copy(rows[:, F_SRC, :], rows_i[:, 0, :]))
                    L.do(nc.vector.tensor_copy(rows[:, F_DST, :], rows_i[:, 1, :]))
                    L.do(nc.vector.tensor_scalar(tmp_i[:, 0, :], rows_i[:, 1, :], 127, None, ALU.bitwise_and))
                    L.do(nc.vector.tensor_scalar(tmp_i[:, 1, :], rows_i[:, 1, :], 7, None, ALU.logical_shift_right))
                    L.wait()
                    L.do(nc.vector.tensor_copy(rows[:, F_LO, :], tmp_i[:, 0, :]))
                    L.do(nc.vector.tensor_copy(rows[:, 6, :], tmp_i[:, 1, :]))
                    for k, f in ((2, F_I3), (3, F_I8)):
                        L.do(nc.vector.scalar_tensor_tensor(rows[:, f, :], rows_i[:, k, :], float(NP),
                                                            rows[:, F_SRC, :], ALU.mult, ALU.add))
                    L.wait()
                    e.sem_inc(s_r, 1)
                    for f in range(7):
                        e.wait_ge(s_t, f + 1)
                        o = hi_c[:, :] if f == 6 else R[:, :, f]
                        L.do(nc.vector.tensor_copy(o, ptr[f][:, 0:EJ]))
                    L.wait()
                    L.step(nc.vector.tensor_tensor(oh_hi[:, :, :], bc(iota_row[0:EP, 0:T], 1, EJ), bc(hi_c[:, :], 2, T),
                                                   ALU.is_equal))

                @blk.tensor
                def _(e):
                    e.wait_ge(s_r, 1)
                    for f in range(7):
                        for g in range(RG):
                            last = nc.tensor.transpose(ptr[f][:, g * RP:(g + 1) * RP],
                                                       rows[:, f, g * EP:(g + 1) * EP], ident[0:RP, 0:RP])
                        last.then_inc(s_t, 1)

        with stage() as s:
            oh = s.sb("oh", [EP, 2, SORT_J, P], BF16)
            pc = [s.ps(f"pc{k}", [P, 512]) for k in range(2)]
            s_o, s_m, s_e = (s.sem(n) for n in ("o", "m", "e"))
            with nc.Block() as blk:
                @blk.vector
                def _(e):
                    e.sem_inc(s_m, 2)

                    def step(u, par, i):
                        e.wait_ge(s_m, u + 1)
                        nc.vector.tensor_tensor(oh[:, par, :, :], bc(iota_row[0:EP, :], 1, SORT_J),
                                                bc(R[:, bass.ds(u * SORT_J, SORT_J), F_LO], 2, P), ALU.is_equal
                                                ).then_inc(s_o, 1)
                    steps(e, NSORT, step)

                @blk.tensor
                def _(e):
                    def step(u, par, i):
                        e.wait_ge(s_o, u + 1)
                        e.wait_ge(s_e, u + 1)
                        for k in range(SORT_J):
                            last = nc.tensor.matmul(pc[par][:, k * T:(k + 1) * T], oh[:, par, k, :],
                                                    oh_hi[:, bass.ds(u * SORT_J + k, 1), :].rearrange("p a t -> p (a t)"),
                                                    start=True, stop=True)
                        last.then_inc(s_m, 1)
                    steps(e, NSORT, step)

                @blk.scalar
                def _(e):
                    e.sem_inc(s_e, 2)

                    def step(u, par, i):
                        e.wait_ge(s_m, u + 3)
                        nc.scalar.copy(cnt[:, :, bass.ds(u * SORT_J, SORT_J)],
                                       pc[par][:, 0:SORT_J * T].rearrange("p (j t) -> p t j", t=T)).then_inc(s_e, 1)
                    steps(e, NSORT, step)

        with stage() as s:
            tot = s.sb("tot", [P, T])
            base = s.sb("base", [P, T])
            pairs_i = s.sb("pairs_i", [P, T], I32)
            pairs = s.sb("pairs", [P, T])
            pend = s.sb("pend", [P, T + 1])
            pref = s.sb("pref", [P, T, EJ])
            upper = s.sb("upper", [P, P])
            ones = s.sb("ones", [P, P])
            q_i = s.sb("q_i", [1, PAIRS], I32)
            q_f = s.sb("q_f", [1, PAIRS])
            q_ge = pref[0:1, :, :].rearrange("p t j -> p (t j)")[:, 0:PAIRS * T].rearrange("p (q t) -> p q t", t=T)
            pt = s.ps("pt", [P, 512])
            s_v, s_u, s_t, s_m, s_pr, s_pa = (s.sem(n) for n in ("v", "u", "t", "m", "pr", "pa"))
            with nc.Block() as blk:
                @blk.scalar
                def _(e):
                    for t in range(T):
                        if t % 5 == 0:
                            e.wait_ge(s_pr, t // 5 + 1)
                        nc.scalar.copy(pa[:, :, t], pref[:, t, :]).then_inc(s_pa, 1)

                @blk.gpsimd
                def _(e):
                    nc.gpsimd.memset(upper[:, :], 1.0).then_inc(s_u, 1)
                    nc.gpsimd.memset(ones[:, :], 1.0).then_inc(s_u, 1)
                    nc.gpsimd.iota(q_i[:, :], pattern=[[1, PAIRS]], base=0, channel_multiplier=0).then_inc(s_u, 1)
                    e.wait_ge(s_u, 3)
                    nc.gpsimd.affine_select(out=upper[:, :], in_=upper[:, :], compare_op=ALU.is_gt, fill=0.0,
                                            base=0, pattern=[[1, P]], channel_multiplier=-1).then_inc(s_u, 1)

                @blk.tensor
                def _(e):
                    e.wait_ge(s_u, 4)
                    e.wait_ge(s_t, 1)
                    nc.tensor.matmul(pt[:, 0:T], upper[:, :], tot[:, :], start=True, stop=True)
                    nc.tensor.matmul(pt[:, T:2 * T], ones[:, :], tot[:, :], start=True, stop=True).then_inc(s_m, 1)

                @blk.vector
                def _(e):
                    L = Link(e, s_v)
                    nc.vector.tensor_reduce(tot[:, :], cnt[:, :, :], AX.X, ALU.add).then_inc(s_t, 1)
                    e.wait_ge(s_m, 1)
                    L.step(nc.vector.tensor_scalar(pairs_i[:, :], pt[:, T:2 * T], 255.0, None, ALU.add))
                    L.step(nc.vector.tensor_scalar(pairs_i[:, :], pairs_i[:, :], 8, None, ALU.logical_shift_right))
                    L.do(nc.vector.tensor_copy(pairs[:, :], pairs_i[:, :]))
                    L.do(nc.vector.memset(base[:, :], 0.0))
                    L.do(nc.vector.memset(pend[:, :], 0.0))
                    L.wait()
                    L.step(nc.vector.tensor_tensor_scan(pend[:, 1:T + 1], base[:, :], pairs[:, :], 0.0, ALU.add, ALU.add))
                    L.do(nc.vector.scalar_tensor_tensor(base[:, :], pend[:, 0:T], 256.0, pt[:, 0:T], ALU.mult, ALU.add))
                    e.wait_ge(s_u, 4)
                    L.do(nc.vector.tensor_copy(q_f[:, :], q_i[:, :]))
                    L.wait()
                    L.step(nc.vector.tensor_tensor(q_ge, bc(q_f[:, :], 2, T), bc(pend[0:1, 1:T + 1], 1, PAIRS), ALU.is_ge))
                    L.step(nc.vector.tensor_reduce(q_f[:, :], q_ge, AX.X, ALU.add))
                    L.do(nc.vector.tensor_scalar(tile_q[:, 0:PAIRS], q_f[:, :], float(T - 1), None, ALU.min))
                    L.wait()
                    L.step(nc.vector.tensor_copy(pref[:, :, 0], base[:, :]))
                    for t in range(T):
                        L.do(nc.vector.tensor_tensor_scan(pref[:, t, 1:EJ], cnt[:, t, 0:EJ - 1], cnt[:, t, 0:EJ - 1],
                                                          base[:, t:t + 1], ALU.add, ALU.max))
                        if t % 5 == 4:
                            L.wait()
                            e.sem_inc(s_pr, 1)
                    e.wait_ge(s_pa, T)
                    L.step(nc.vector.tensor_tensor(pb[:, :, :].rearrange("p j t -> p t j"), pref[:, :, :],
                                                   pa[:, :, :].rearrange("p j t -> p t j"), ALU.subtract))

        counting.close()

        with stage() as s:
            drow = s.sb("drow", [EP, 2, SORT_J, EP], I32)
            oh = s.sb("oh", [EP, SORT_J, P], BF16)
            oht = s.sb("oht", [P, SORT_J, P], BF16)
            tri = s.sb("tri", [EP, EP])
            eq = s.sb("eq", [EP, SORT_J, EP], BF16)
            dcol = s.sb("dcol", [EP, SORT_J])
            same = s.sb("same", [EP, SORT_J])
            sel = s.sb("sel", [EP, SORT_J, T])
            spos = s.sb("spos", [EP, SORT_J])
            slot = s.sb("slot", [EP, 2, SORT_J], I32)
            recs = s.sb("recs", [EP, 2, SORT_J, REC])
            pt = [s.ps(f"pt{k}", [P, 8, P], BF16) for k in range(3)]
            pl = s.ps("pl", [EP, 512])
            s_tri, s_o, s_t, s_a, s_l, s_v, s_f, s_r, s_go, s_out = (
                s.sem(n) for n in ("tri", "o", "t", "a", "l", "v", "f", "r", "go", "out"))
            s_d = [s.sem("d0"), s.sem("d1")]
            s_s = [s.sem("s0"), s.sem("s1")]
            with nc.Block() as blk:
                @blk.sync
                def _(e):
                    def load(u, par, i):
                        e.wait_ge(s_f, u + 1)
                        e.dma_start(drow[:, par, :, :].rearrange("p j e -> p (j e)"),
                                    io["dst"][bass.ds(u * (SORT_J * EP), SORT_J * EP)].unsqueeze(0)
                                    .to_broadcast([EP, SORT_J * EP])).then_inc(s_d[par], 16)
                    steps(e, NSORT, load)

                @blk.tensor
                def _(e):
                    with e.Fori(0, NSORT) as i:
                        e.wait_ge(s_o, i + 1)
                        for k in range(SORT_J):
                            last = nc.tensor.transpose(pt[k // 8][:, k % 8, 0:EP], oh[:, k, :], ident_b[0:EP, 0:EP])
                        last.then_inc(s_t, 1)
                        e.wait_ge(s_a, i + 1)
                        e.wait_ge(s_f, i + 2)
                        for k in range(SORT_J):
                            for n, part in enumerate((pa, pb)):
                                last = nc.tensor.matmul(pl[:, k * T:(k + 1) * T], oht[:, k, 0:EP],
                                                        part[:, bass.ds(i * SORT_J + k, 1), :].rearrange("p a t -> p (a t)"),
                                                        start=(n == 0), stop=(n == 1))
                        last.then_inc(s_l, 1)

                @blk.scalar
                def _(e):
                    with e.Fori(0, NSORT) as i:
                        e.wait_ge(s_t, i + 1)
                        for k in range(3):
                            m = min(8, SORT_J - 8 * k)
                            last = nc.scalar.copy(oht[:, 8 * k:8 * k + m, 0:EP], pt[k][:, 0:m, 0:EP])
                        last.then_inc(s_a, 1)

                @blk.vector
                def _(e):
                    e.sem_inc(s_f, 2)
                    e.sem_inc(s_out, 2)
                    L = Link(e, s_v)
                    e.wait_ge(s_tri, 2)
                    per = 6 + SORT_J

                    def place(u, par, i):
                        L.i, L.per, L.n = u, per, 0
                        j0 = u * SORT_J
                        L.do(nc.vector.tensor_copy(dcol[:, :], R[:, bass.ds(j0, SORT_J), F_DST]))
                        L.do(nc.vector.tensor_tensor(oh[:, :, :], bc(iota_row[0:EP, :], 1, SORT_J),
                                                     bc(R[:, bass.ds(j0, SORT_J), F_LO], 2, P), ALU.is_equal))
                        L.wait()
                        e.sem_inc(s_o, 1)
                        e.wait_ge(s_d[par], i * 16 + 16)
                        for k in range(SORT_J):
                            L.do(nc.vector.scalar_tensor_tensor(eq[:, k, :], drow[:, par, k, :], dcol[:, k:k + 1], tri[:, :],
                                                                ALU.is_equal, ALU.mult, accum_out=same[:, k:k + 1]))
                        e.wait_ge(s_l, u + 1)
                        L.step(nc.vector.tensor_tensor(sel[:, :, :], pl[:, 0:SORT_J * T].rearrange("p (j t) -> p j t", t=T),
                                                       oh_hi[:, bass.ds(j0, SORT_J), :], ALU.mult))
                        L.step(nc.vector.tensor_reduce(spos[:, :], sel[:, :, :], AX.X, ALU.add))
                        e.sem_inc(s_f, 1)
                        e.wait_ge(s_out, u + 1)
                        L.do(nc.vector.tensor_tensor(slot[:, par, :], spos[:, :], same[:, :], ALU.add))
                        L.do(nc.vector.tensor_copy(recs[:, par, :, :], R[:, bass.ds(j0, SORT_J), :]))
                        L.wait()
                        e.sem_inc(s_r, 1)
                        assert L.n == per, L.n
                    steps(e, NSORT, place)

                @blk.gpsimd
                def _(e):
                    nc.gpsimd.memset(tri[:, :], 1.0).then_inc(s_tri, 1)
                    e.wait_ge(s_tri, 1)
                    nc.gpsimd.affine_select(out=tri[:, :], in_=tri[:, :], compare_op=ALU.is_gt, fill=0.0, base=0,
                                            pattern=[[-1, EP]], channel_multiplier=1).then_inc(s_tri, 1)
                    per_step = 16 * SORT_J

                    def scatter(u, par):
                        e.wait_ge(s_r, u + 1)
                        e.sem_inc(s_go, 1)
                        for k in range(SORT_J):
                            nc.gpsimd.indirect_dma_start(
                                out=rec, out_offset=bass.IndirectOffsetOnAxis(ap=slot[:, par, k:k + 1], axis=0),
                                in_=recs[:, par, k, :], in_offset=None).then_inc(s_s[par], 16)

                    scatter(0, 0)
                    with e.Fori(0, NSORT // 2) as i:
                        scatter(i * 2 + 1, 1)
                        e.wait_ge(s_s[0], i * per_step + per_step)
                        e.sem_inc(s_out, 1)
                        scatter(i * 2 + 2, 0)
                        e.wait_ge(s_s[1], i * per_step + per_step)
                        e.sem_inc(s_out, 1)
                    e.wait_ge(s_s[0], per_step * ((NSORT + 1) // 2))

    H = keep("H", [P, T + 1, D])
    acc = keep("acc", [P, T + 1, W8])
    pen = keep("pen", [P, NW, P + 1], BF16)
    conn = keep("conn", [1, CH + 1], BF16)
    single = keep("single", [1, CH], BF16)

    NT = 4
    masks = keep("masks", [P, T, NT])
    with stage() as s:
        ty_i = s.sb("ty_i", [T, P], I32)
        ty_r = s.sb("ty_r", [T, P])
        ty = s.sb("ty", [P, T])
        pt = s.ps("pt", [P, 512])
        s_in, s_z, s_v, s_t = (s.sem(n) for n in ("in", "z", "v", "t"))
        with nc.Block() as blk:
            @blk.sync
            def _(e):
                e.wait_ge(s_z, 1)
                e.dma_start(ty_i[0:T - 1, :], io["node_type_4"][0:(T - 1) * P].rearrange("(t p) -> t p", p=P)).then_inc(s_in, 16)
                e.dma_start(ty_i[T - 1:T, 0:TAIL], io["node_type_4"][(T - 1) * P:N].unsqueeze(0)).then_inc(s_in, 16)

            @blk.tensor
            def _(e):
                e.wait_ge(s_v, 1)
                nc.tensor.transpose(pt[:, 0:T], ty_r[:, :], ident[0:T, 0:T]).then_inc(s_t, 1)

            @blk.vector
            def _(e):
                L = Link(e, s_v)
                nc.vector.memset(ty_i[:, :], 0).then_inc(s_z, 1)
                e.wait_ge(s_in, 32)
                L.do(nc.vector.tensor_copy(ty_r[:, :], ty_i[:, :]))
                e.wait_ge(s_t, 1)
                for t in range(NT):
                    L.do(nc.vector.tensor_scalar(masks[:, :, t], pt[:, 0:T], float(t), None, ALU.is_equal))

    with stage() as s:
        rt = s.sb("rt", [LP, LG, P * REC])
        dstc = s.sb("dstc", [P, CH])
        idx8_c = s.sb("idx8_c", [P, CH], I32)
        w_c = s.sb("w_c", [P, CH])
        dsth = s.sb("dsth", [P, CH, HD])
        grp = s.sb("grp", [P, NW, P])
        lastd = s.sb("lastd", [1, CH])
        ptr = [s.ps(f"ptr{k}", [P, 512]) for k in range(8)]
        s_in, s_t, s_v, s_x, s_g, s_y, s_r = (s.sem(n) for n in ("in", "t", "v", "x", "g", "y", "r"))
        banks = -(-NW // 4)
        with nc.Block() as blk:
            @blk.sync
            def _(e):
                e.dma_start(rt[:, :, :], rec.rearrange("(g p e) f -> p g (e f)", g=LG, p=LP)).then_inc(s_in, 16)
                e.wait_ge(s_y, 1)
                e.dma_start(keep_i8, idx8_c[:, :]).then_inc(s_r, 16)
                e.dma_start(keep_w, w_c[:, :]).then_inc(s_r, 16)
                e.dma_start(lastd[:, :], dstc[P - 1:P, :]).then_inc(s_r, 16)
                e.wait_ge(s_r, 48)

            @blk.tensor
            def _(e):
                e.wait_ge(s_in, 16)
                for f in range(6):
                    for g in range(LG):
                        last = nc.tensor.transpose(ptr[f][:, g * LP:(g + 1) * LP],
                                                   rt[:, g, :].rearrange("p (e f) -> p f e", f=REC)[:, f, :],
                                                   ident[0:LP, 0:LP])
                    last.then_inc(s_t, 1)
                e.wait_ge(s_x, 1)
                for w in range(NW):
                    last = nc.tensor.transpose(ptr[w // 4][:, (w % 4) * P:(w % 4 + 1) * P],
                                               dsth[:, w * WC:(w + 1) * WC, :].rearrange("p c h -> p (c h)"), ident[:, :])
                    if w % 4 == 3 or w == NW - 1:
                        last.then_inc(s_g, 1)

            @blk.vector
            def _(e):
                L = Link(e, s_v)
                L.do(nc.vector.memset(H[:, T - 1:, :], 0.0))
                L.do(nc.vector.memset(acc[:, T:, :], 0.0))
                L.do(nc.vector.memset(pen[:, :, :], 0.0))
                L.do(nc.vector.memset(conn[:, :], -BIG))
                for f, o in enumerate((src_i, idx3_i, idx8_c, w_c, lo_s, dstc)):
                    e.wait_ge(s_t, f + 1)
                    L.do(nc.vector.tensor_copy(o[:, 0:CH], ptr[f][:, 0:CH]))
                L.wait()
                e.sem_inc(s_y, 1)
                L.step(nc.vector.tensor_copy(dsth[:, :, :], bc(dstc[:, :], 2, HD)))
                e.sem_inc(s_x, 1)
                for k in range(banks):
                    n = min(4, NW - 4 * k)
                    e.wait_ge(s_g, k + 1)
                    L.do(nc.vector.tensor_copy(grp[:, 4 * k:4 * k + n, :].rearrange("p w e -> p (w e)"), ptr[k][:, 0:n * P]))
                L.wait()
                L.step(nc.vector.tensor_tensor(pen[:, :, 1:P], grp[:, :, 0:P - 1], grp[:, :, 1:P], ALU.not_equal))
                L.do(nc.vector.tensor_scalar(pen[:, :, 1:P], pen[:, :, 1:P], -BIG, None, ALU.mult))
                e.wait_ge(s_r, 48)
                L.do(nc.vector.tensor_tensor(conn[:, 1:CH], lastd[:, 0:CH - 1], dstc[0:1, 1:CH], ALU.not_equal))
                L.do(nc.vector.tensor_tensor(single[:, :], lastd[:, :], dstc[0:1, :], ALU.not_equal))
                L.wait()
                L.do(nc.vector.tensor_scalar(conn[:, 1:CH], conn[:, 1:CH], -BIG, None, ALU.mult))
                L.do(nc.vector.tensor_scalar(single[:, :], single[:, :], -BIG, None, ALU.mult))
                L.wait()

    def gather(e, ring, islot, idx, table, s_free, s_is, s_go, s_g):
        def step(u, par, i):
            e.wait_ge(s_free, u + 1)
            e.sem_inc(s_go, 1)
            nc.gpsimd.tensor_copy(islot[:, par, :], idx[:, bass.ds(u * BODY, BODY)]).then_inc(s_is, 1)
            e.wait_ge(s_is, u + 1)
            e.sem_inc(s_go, 1)
            for k in range(BODY):
                nc.gpsimd.indirect_dma_start(
                    out=ring[:, par, k, :], out_offset=None, in_=table,
                    in_offset=bass.IndirectOffsetOnAxis(ap=islot[:, par, k:k + 1], axis=0)).then_inc(s_g[par], 16)
        steps(e, NBODY, step)

    def tiles_of(e_type, u):
        _, vals = nc.values_load_multi_w_load_instructions(
            tile_q[0:1, bass.ds(u * (BODY // 2), BODY // 2)], engines=[e_type], min_val=0, max_val=T - 1,
            skip_runtime_bounds_check_because="they come from a minimum with T - 1")
        return vals

    def windows(first, both, last, e):
        first(0, 0, 1)
        with e.Fori(0, NW // 2) as i:
            both(i * 2 + 1, 1, i + 1)
            both(i * 2 + 2, 0, i + 2)
        last(NW - 1, 0)

    def order(text):
        return [(x[0], int(x[1:] or 0)) for x in text.split()]
    ORDER_V_DOTS = order("S0 S1 W0 S2 W1 t S3 W2 A0 S4 W3 A1 S5 S6 A2 S7 W4 A3 W5 D1 A4 W6 D2 A5 W7 A6 D3 A7")
    ORDER_V_SUMS = order("W0 W1 t W2 A0 W3 A1 W4 A2 A3 L W5 D1 A4 W6 D2 A5 W7 A6 D3 A7")
    ORDER_T_DOTS = order("Q2 Q3 G0 T2 G1 Q4 Q5 T3 G2 Q6 Q7 G3 C1 G4 C2 G5 G6 C3 N0 N1 G7 H C4")
    ORDER_T_SUMS = order("G0 Q2 Q3 G1 T2 G2 Q4 Q5 T3 G3 Q6 Q7 C1 G4 C2 G5 G6 C3 N0 N1 G7 H C4")

    def attend(Qs, heads, row, at_k, idx, table, scratch):
        dots = heads == HD
        order_v = ORDER_V_DOTS if dots else ORDER_V_SUMS
        order_t = ORDER_T_DOTS if dots else ORDER_T_SUMS
        width = D if dots else HD
        with stage() as s:
            ring = s.sb("ring", [P, 2, WC, row])
            islot = s.sb("islot", [P, 2, WC], I32)
            oh = scratch[:, 0:2 * WC * P].rearrange("p (b c n) -> p b c n", b=2, c=WC)
            if dots:
                prod = scratch[:, 2 * WC * P:2 * WC * P + 4 * 2 * D].rearrange("p (k c d) -> p k c d", k=4, c=2)
            ohb = s.sb("ohb", [P, 2, 4, P], BF16)
            oht = s.sb("oht", [P, 2, 4, P], BF16)
            scw = s.sb("scw", [P, 2, WC, HD])
            S1, F, R = (scratch[:, scratch.shape[1] - (k + 1) * P:scratch.shape[1] - k * P] for k in range(3))
            penw = s.sb("penw", [P, P + 1], BF16)
            cc = s.sb("cc", [P, 2])
            fac = s.sb("fac", [P, HD])
            rF = s.sb("rF", [1, HD, WC + 1])
            rB = s.sb("rB", [1, HD, WC])
            pL = s.sb("pL", [1, HD, WC + 1])
            pR = s.sb("pR", [1, HD, WC])
            cL = s.sb("cL", [1, HD, WC + 1])
            cR = s.sb("cR", [1, HD, WC])
            inL = s.sb("inL", [1, WC, HD])
            inR = s.sb("inR", [1, WC, HD])
            gr = s.sb("gr", [1, HD])
            pt = [s.ps(f"pt{k}", [P, 8, P], BF16) for k in range(2)]
            pq = [s.ps(f"pq{k}", [P, 512]) for k in range(2)]
            pp = [s.ps(f"pp{k}", [P, 512]) for k in range(2)]
            pc = [s.ps(f"pc{k}", [P, 512]) for k in range(2)]
            (s_is, s_go, s_oh, s_tr, s_ev, s_q, s_mul, s_red, s_T1, s_S1, s_FB, s_T2, s_rows, s_eg, s_T3, s_sub, s_g1,
             s_exp, s_T4, s_fac, s_ex, s_m, s_pp, s_acc, s_d, s_ma, s_g1b, s_ab, s_mp) = (s.sem(n) for n in (
                 "is", "go", "oh", "tr", "ev", "q", "mul", "red", "T1", "S1", "FB", "T2", "rows", "eg", "T3", "sub", "g1",
                 "exp", "T4", "fac", "ex", "m", "pp", "acc", "d", "ma", "bwd", "ab", "mp"))
            s_g = [[s.sem(f"g{b}{q}") for q in range(4)] for b in range(2)]
            NQ = WC // 4
            NPR = WC // 2
            on_pool = (3, 5, 7) if dots else ()
            on_dve = [p for p in range(NPR) if p not in on_pool]

            def weigh_pair(eng, par, p):
                v = ring[:, par, 2 * p:2 * p + 2, 0:D].rearrange("p c (h x) -> p c h x", h=heads)
                return eng.tensor_tensor(v, v, bc(ring[:, par, 2 * p:2 * p + 2, D:D + heads], 3, D // heads), ALU.mult)
            exs = lambda par: ring[:, par, :, D:W8]

            with nc.Block() as blk:
                @blk.gpsimd
                def _(e):
                    def weigh(w, par, k):
                        e.wait_ge(s_ex, w + 1)
                        e.sem_inc(s_go, 1)
                        weigh_pair(nc.gpsimd, par, on_pool[k]).then_inc(s_mp, 1)

                    def step(w, par, before):
                        if before and on_pool:
                            weigh(w - 2, par, 0)
                        e.wait_ge(s_pp, w * NPR + 2)
                        e.sem_inc(s_go, 1)
                        nc.gpsimd.tensor_copy(islot[:, par, :], idx[:, bass.ds(w * WC, WC)]).then_inc(s_is, 1)
                        e.wait_ge(s_is, w + 1)
                        e.sem_inc(s_go, 1)
                        for q in range(NQ):
                            if before and 0 < q < len(on_pool):
                                weigh(w - 2, par, q)
                            e.wait_ge(s_pp, w * NPR + (2 * q + 2))
                            e.sem_inc(s_go, 1)
                            for c in range(4 * q, 4 * q + 4):
                                nc.gpsimd.indirect_dma_start(
                                    out=ring[:, par, c, :], out_offset=None, in_=table,
                                    in_offset=bass.IndirectOffsetOnAxis(ap=islot[:, par, c:c + 1], axis=0)
                                    ).then_inc(s_g[par][q], 16)
                    step(0, 0, False)
                    step(1, 1, False)
                    with e.Fori(0, (NW - 3) // 2) as i:
                        step(i * 2 + 2, 0, True)
                        step(i * 2 + 3, 1, True)
                    step(NW - 1, 0, True)
                    for w, par in ((NW - 2, 1), (NW - 1, 0)):
                        for k in range(len(on_pool)):
                            weigh(w, par, k)

                @blk.tensor
                def _(e):
                    e.sem_inc(s_pp, 2 * NPR)

                    def tiles8(q0):
                        return nc.values_load_multi_w_load_instructions(
                            tile_q[0:1, bass.ds(q0, NPR)], engines=[mybir.EngineType.PE], min_val=0, max_val=T - 1,
                            skip_runtime_bounds_check_because="they come from a minimum with T - 1")[1]

                    def transposes(w, q):
                        e.wait_ge(s_oh, w * (2 * NQ) + (2 * q + 2))
                        for c in range(4):
                            last = nc.tensor.transpose(pt[q % 2][:, c, :], ohb[:, q % 2, c, :], ident_b[:, :])
                        last.then_inc(s_tr, 1)

                    def qrow(w, par, tl, p):
                        q = p // 2
                        tile_ = tl[0] if p > 1 else tl[p]
                        e.wait_ge(s_ev, w * NQ + (q + 1))
                        if dots:
                            e.wait_ge(s_mul, w * NPR + (p + 1))
                        elif p == 0:
                            e.wait_ge(s_red, w + 1)
                        for c in range(2):
                            if dots:
                                o = pq[p % 2][:, c * D:(c + 1) * D]
                            else:
                                o = pq[par][:, (2 * p + c) * HD:(2 * p + c + 1) * HD]
                            for r in range(3):
                                last = nc.tensor.matmul(o, oht[:, q % 2, 2 * (p % 2) + c, :],
                                                        Qs[:, bass.ds(tile_, 1), r, :].rearrange("p a d -> p (a d)"),
                                                        start=(r == 0), stop=(r == 2))
                        last.then_inc(s_q, 1)

                    def T1(w, par):
                        e.wait_ge(s_red, (w * NPR + (4 + NPR)) if dots else w + 3)
                        nc.tensor.transpose(pc[0][:, 0:P], scw[:, par, :, :].rearrange("p c h -> p (c h)"), ident[:, :]
                                            ).then_inc(s_T1, 1)

                    def T2(w, par):
                        e.wait_ge(s_FB, w * 2 + 2)
                        nc.tensor.transpose(pc[1][0:1, 0:P], F[:, P - 1:P], ident[:, :])
                        nc.tensor.transpose(pc[1][0:1, P:2 * P], R[:, 0:1], ident[:, :]).then_inc(s_T2, 1)

                    def T3(w, par):
                        e.wait_ge(s_rows, w + 1)
                        e.sem_inc(s_go, 1)
                        nc.tensor.transpose(pc[1][:, 256:257], inL[:, :, :].rearrange("o c h -> o (c h)"), ident[0:1, 0:1])
                        nc.tensor.transpose(pc[1][:, 257:258], inR[:, :, :].rearrange("o c h -> o (c h)"), ident[0:1, 0:1]
                                            ).then_inc(s_T3, 1)

                    def T4(w, par):
                        e.wait_ge(s_exp, w + 1)
                        nc.tensor.matmul(pc[1][:, 264:264 + HD], oh[0:1, par, 0, :], gr[:, :], start=True, stop=True
                                         ).then_inc(s_fac, 1)
                        nc.tensor.transpose(pc[0][:, 0:P], S1[:, :], ident[:, :]).then_inc(s_T4, 1)

                    def agg(w, par, p):
                        if p in on_dve:
                            e.wait_ge(s_m, w * len(on_dve) + (on_dve.index(p) + 1))
                        else:
                            e.wait_ge(s_mp, w * len(on_pool) + (on_pool.index(p) + 1))
                        e.wait_ge(s_acc, w * NPR + (p + 1))
                        for c in range(2):
                            last = nc.tensor.matmul(pp[p % 2][:, 0:W8], oh[:, par, 2 * p + c, :],
                                                    ring[:, par, 2 * p + c, 0:W8], start=(c == 0), stop=(c == 1))
                        last.then_inc(s_pp, 1)

                    def ahead(w, par, tl):
                        qrow(w, par, tl, 0)
                        qrow(w, par, tl, 1)

                    def first(w, par, n):
                        transposes(w, 0)
                        transposes(w, 1)
                        ahead(w, par, tiles8(w * NPR))
                        tl = tiles8(w * NPR + 2)
                        for p in range(2, NPR):
                            if p in (2, 4):
                                transposes(w, p // 2 + 1)
                            qrow(w, par, tl[p - 2:], p)
                        T1(w, par)
                        T2(w, par)
                        T3(w, par)
                        transposes(w + 1, 0)
                        transposes(w + 1, 1)
                        T4(w, par)
                        ahead(w + 1, 1 - par, tl[NPR - 2:])

                    def both(w, par, n):
                        tl = tiles8(w * NPR + 2)
                        for kind, p in order_t:
                            if kind == "Q":
                                qrow(w, par, tl[p - 2:], p)
                            elif kind == "G":
                                agg(w - 1, 1 - par, p)
                            elif kind == "T":
                                transposes(w, p)
                            elif kind == "N":
                                transposes(w + 1, p)
                            elif kind == "H":
                                ahead(w + 1, 1 - par, tl[NPR - 2:])
                            elif kind == "C":
                                (T1, T2, T3, T4)[p - 1](w, par)

                    def last_(w, par):
                        for p in range(NPR):
                            agg(w, par, p)
                    windows(first, both, last_, e)

                @blk.scalar
                def _(e):
                    def onehots(w, par, q):
                        e.wait_ge(s_pp, w * NPR + (2 * q + 2))
                        for c in range(4):
                            last = nc.scalar.activation(ohb[:, q % 2, c, :], iota_row[:, :], ACT.Abs, scale=-1.0,
                                                        bias=lo_s[:, bass.ds(w * WC + (4 * q + c), 1)])
                        last.then_inc(s_ab, 1)
                        e.wait_ge(s_ab, w * NQ + (q + 1))
                        nc.scalar.activation(oh[:, par, 4 * q:4 * q + 4, :], ohb[:, q % 2, :, :], ACT.Relu, scale=-1.0, bias=1.0
                                             ).then_inc(s_oh, 1)
                        e.wait_ge(s_oh, w * (2 * NQ) + (2 * q + 1))
                        nc.scalar.activation(ohb[:, q % 2, :, :], ohb[:, q % 2, :, :], ACT.Relu, scale=-1.0, bias=1.0
                                             ).then_inc(s_oh, 1)

                    def evacuate(w, q):
                        e.wait_ge(s_tr, w * NQ + (q + 1))
                        nc.scalar.copy(oht[:, q % 2, :, :], pt[q % 2][:, 0:4, :]).then_inc(s_ev, 1)

                    def rest(w, par):
                        onehots(w, par, 2)
                        if dots:
                            evacuate(w, 2)
                            onehots(w, par, 3)
                        else:
                            onehots(w, par, 3)
                            evacuate(w, 2)
                        evacuate(w, 3)
                        if dots:
                            onehots(w + 1, 1 - par, 0)
                        e.wait_ge(s_T1, w + 1)
                        nc.scalar.copy(S1[:, :], pc[0][:, 0:P]).then_inc(s_S1, 1)
                        if not dots:
                            onehots(w + 1, 1 - par, 0)
                        onehots(w + 1, 1 - par, 1)
                        e.wait_ge(s_rows, w + 1)
                        nc.scalar.activation(gr[:, :], gr[:, :], ACT.Exp).then_inc(s_eg, 1)
                        evacuate(w + 1, 0)
                        evacuate(w + 1, 1)
                        e.wait_ge(s_sub, w + 1)
                        nc.scalar.activation(S1[:, :], S1[:, :], ACT.Exp).then_inc(s_exp, 1)
                        e.wait_ge(s_T4, w + 1)
                        nc.scalar.copy(exs(par), pc[0][:, 0:P].rearrange("p (c h) -> p c h", h=HD)).then_inc(s_ex, 1)

                    def first(w, par, n):
                        for q in range(2):
                            onehots(w, par, q)
                        for q in range(2):
                            evacuate(w, q)
                        rest(w, par)
                    windows(first, lambda w, par, n: rest(w, par), lambda w, par: None, e)

                @blk.vector
                def _(e):
                    C, M = Link(e, s_d), Link(e, s_ma)
                    e.sem_inc(s_mul, 2)
                    e.sem_inc(s_red, 4 if dots else 2)
                    e.sem_inc(s_acc, 2)
                    C.do(nc.vector.memset(acc[:, 0:T, :], 0.0))
                    C.do(nc.vector.memset(rF[:, :, :], -BIG))
                    C.do(nc.vector.memset(pL[:, :, :], -BIG))
                    C.do(nc.vector.memset(pR[:, :, :], -BIG))
                    C.do(nc.vector.memset(inR[:, :, :], -BIG))
                    C.wait()
                    c_base, c_per, m_per = C.n, 15, 3
                    cw = lambda w, a=0, n=WC: conn[:, bass.ds(w * WC + a, n)]
                    hb = lambda ap: bc(ap, 1, HD)
                    hc = lambda ap: ap.rearrange("o (c h) -> o h c", h=HD)

                    def red(w, par, p):
                        e.wait_ge(s_mul, w * NPR + (p + 3))
                        nc.vector.tensor_reduce(scw[:, par, 2 * p:2 * p + 2, :],
                                                prod[:, p % 4, :, :].rearrange("p c (h x) -> p c h x", h=HD),
                                                AX.X, ALU.add).then_inc(s_red, 1)

                    def dot(w, par, n, p):
                        if p % 2 == 0:
                            e.wait_ge(s_g[par][p // 2], n * 64)
                        e.wait_ge(s_q, w * NPR + (p + 1))
                        e.wait_ge(s_red, w * NPR + (p + 1))
                        nc.vector.tensor_tensor(prod[:, p % 4, :, :], ring[:, par, 2 * p:2 * p + 2, at_k:at_k + D],
                                                pq[p % 2][:, :].rearrange("p (c d) -> p c d", c=2), ALU.mult
                                                ).then_inc(s_mul, 1)
                        if p:
                            red(w, par, p - 1)
                        if p == NPR - 1:
                            red(w, par, p)

                    def leaky(w, par, n):
                        for q in range(NQ):
                            e.wait_ge(s_g[par][q], n * 64)
                        e.wait_ge(s_q, w * NPR + NPR)
                        nc.vector.tensor_tensor(scw[:, par, :, :], ring[:, par, :, at_k:at_k + HD],
                                                pq[par][:, 0:P].rearrange("p (c h) -> p c h", h=HD), ALU.add
                                                ).then_inc(s_mul, 1)
                        e.wait_ge(s_mul, w + 3)
                        nc.vector.scalar_tensor_tensor(scw[:, par, :, :], scw[:, par, :, :], 0.2, scw[:, par, :, :],
                                                       ALU.mult, ALU.max).then_inc(s_red, 1)

                    def D1(w):
                        C.i, C.per, C.base, C.n = w, c_per, c_base, 0
                        sg = single[:, bass.ds(w * WC, WC)]
                        C.do(nc.vector.tensor_tensor(pL[:, :, 1:], hb(cw(w)), hb(sg), ALU.add))
                        C.do(nc.vector.tensor_tensor(pR[:, :, 0:WC - 1], hb(cw(w, 1, WC - 1)),
                                                     hb(single[:, bass.ds(w * WC, WC - 1)]), ALU.add))
                        C.do(nc.vector.tensor_copy(penw[:, :], pen[:, bass.ds(w, 1), :].rearrange("p a e -> p (a e)")))
                        C.wait()
                        e.wait_ge(s_S1, w + 1)
                        nc.vector.tensor_tensor_scan(F[:, :], penw[:, 0:P], S1[:, :], -BIG, ALU.add, ALU.max).then_inc(s_FB, 1)
                        nc.vector.tensor_tensor_scan(R[:, ::-1], penw[:, 1:P + 1][:, ::-1], S1[:, ::-1], -BIG, ALU.add, ALU.max
                                                     ).then_inc(s_FB, 1)

                    def D2(w):
                        e.wait_ge(s_T2, w + 1)
                        C.do(nc.vector.tensor_copy(rF[:, :, 1:], hc(pc[1][0:1, 0:P])))
                        C.do(nc.vector.tensor_copy(rB[:, :, :], hc(pc[1][0:1, P:2 * P])))
                        C.wait()
                        flat = lambda a: a.rearrange("o h c -> o (h c)")
                        C.do(nc.vector.tensor_tensor_scan(flat(cR[:, :, :])[:, ::-1], flat(pR[:, :, :])[:, ::-1],
                                                          flat(rB[:, :, :])[:, ::-1], -BIG, ALU.add, ALU.max))
                        C.do(nc.vector.tensor_tensor_scan(flat(cL[:, :, :]), flat(pL[:, :, :]), flat(rF[:, :, :]), -BIG,
                                                          ALU.add, ALU.max))
                        C.wait()
                        C.do(nc.vector.tensor_tensor(inL[:, :, :].rearrange("o c h -> o h c"), cL[:, :, 0:WC], hb(cw(w)), ALU.add))
                        C.do(nc.vector.tensor_tensor(inR[:, 0:WC - 1, :].rearrange("o c h -> o h c"), cR[:, :, 1:],
                                                     hb(cw(w, 1, WC - 1)), ALU.add))
                        C.step(nc.vector.tensor_tensor(gr[:, :], cR[:, :, 0], cw(w, 0, 1).to_broadcast([1, HD]), ALU.add))
                        C.step(nc.vector.tensor_tensor(gr[:, :], rF[:, :, 0], gr[:, :], ALU.subtract))
                        C.do(nc.vector.tensor_scalar(gr[:, :], gr[:, :], 0.0, None, ALU.min))
                        C.do(nc.vector.tensor_copy(rF[:, :, 0], cL[:, :, WC]))
                        C.wait()
                        e.sem_inc(s_rows, 1)

                    def D3(w):
                        e.wait_ge(s_eg, w + 1)
                        nc.vector.tensor_scalar(gr[:, :], gr[:, :], -1.0, None, ALU.add).then_inc(s_g1, 1)
                        e.wait_ge(s_T3, w + 1)
                        C.step(nc.vector.tensor_copy(cc[:, :], pc[1][:, 256:258]))
                        C.step(nc.vector.tensor_tensor_scan(F[:, :], penw[:, 0:P], S1[:, :], cc[:, 0:1], ALU.add, ALU.max))
                        nc.vector.tensor_tensor_scan(R[:, ::-1], penw[:, 1:P + 1][:, ::-1], F[:, ::-1], cc[:, 1:2], ALU.add, ALU.max
                                                     ).then_inc(s_g1b, 1)
                        e.wait_ge(s_g1b, w + 1)
                        nc.vector.tensor_tensor(S1[:, :], S1[:, :], R[:, :], ALU.subtract).then_inc(s_sub, 1)
                        assert C.n == c_per, C.n

                    def rescale(w, tl):
                        M.i, M.per, M.n = w, m_per, 0
                        e.wait_ge(s_fac, w + 1)
                        M.step(nc.vector.tensor_scalar(fac[:, :], pc[1][:, 264:264 + HD], 1.0, None, ALU.add))
                        e.wait_ge(s_acc, w * NPR + 2)
                        a = acc[:, bass.ds(tl[0], 1), :].rearrange("p a d -> p (a d)")
                        av = a[:, 0:D].rearrange("p (h x) -> p h x", h=heads)
                        M.do(nc.vector.tensor_tensor(av, av, bc(fac[:, 0:heads], 2, D // heads), ALU.mult))
                        M.do(nc.vector.tensor_tensor(a[:, D:W8], a[:, D:W8], fac[:, :], ALU.mult))
                        assert M.n == m_per

                    def weigh(w, par, p):
                        if p == 0:
                            e.wait_ge(s_ex, w + 1)
                        if p in on_dve:
                            weigh_pair(nc.vector, par, p).then_inc(s_m, 1)

                    def add(w, tl, p):
                        if p == 0:
                            M.wait()
                        e.wait_ge(s_pp, w * NPR + (p + 1 + 2 * NPR))
                        e.wait_ge(s_acc, w * NPR + (p + 2))
                        a = acc[:, bass.ds(tl[p], 1), :].rearrange("p a d -> p (a d)")
                        nc.vector.tensor_tensor(a, a, pp[p % 2][:, 0:W8], ALU.add).then_inc(s_acc, 1)

                    def tiles8(w):
                        return nc.values_load_multi_w_load_instructions(
                            tile_q[0:1, bass.ds(w * NPR, NPR)], engines=[mybir.EngineType.DVE], min_val=0, max_val=T - 1,
                            skip_runtime_bounds_check_because="they come from a minimum with T - 1")[1]

                    def chain(w):
                        D1(w)
                        D2(w)
                        D3(w)

                    def first(w, par, n):
                        if dots:
                            for p in range(NPR):
                                dot(w, par, n, p)
                        else:
                            leaky(w, par, n)
                        chain(w)

                    def both(w, par, n):
                        for kind, p in order_v:
                            if kind == "t":
                                tl = tiles8(w - 1)
                                rescale(w - 1, tl)
                            elif kind == "W":
                                weigh(w - 1, 1 - par, p)
                            elif kind == "A":
                                add(w - 1, tl, p)
                            elif kind == "D":
                                (D1, D2, D3)[p - 1](w)
                            elif kind == "S" and dots:
                                dot(w, par, n, p)
                            elif kind == "L" and not dots:
                                leaky(w, par, n)

                    def last_(w, par):
                        tl = tiles8(w)
                        rescale(w, tl)
                        for p in range(NPR):
                            weigh(w, par, p)
                            if p:
                                add(w, tl, p - 1)
                        add(w, tl, NPR - 1)
                        e.wait_ge(s_acc, NW * NPR + 2)
                    windows(first, both, last_, e)

    def sum_edges(idx, table, w_s=None):
        with stage() as s:
            ring = s.sb("ring", [P, 2, BODY, D])
            islot = s.sb("islot", [P, 2, BODY], I32)
            oh = s.sb("oh", [P, 2, BODY, P])
            pp = [s.ps(f"pp{k}", [P, 512]) for k in range(4)]
            s_free, s_is, s_go, s_oh, s_p, s_pf, s_v, s_w = (
                s.sem(n) for n in ("free", "is", "go", "oh", "p", "pf", "v", "w"))
            s_g = [s.sem("g0"), s.sem("g1")]
            with nc.Block() as blk:
                @blk.gpsimd
                def _(e):
                    gather(e, ring, islot, idx, table, s_free, s_is, s_go, s_g)

                @blk.tensor
                def _(e):
                    e.sem_inc(s_free, 2)

                    def step(u, par, i):
                        e.wait_ge(s_oh, u + 1)
                        e.wait_ge(s_g[par], i * (16 * BODY) + 16 * BODY)
                        for k in range(BODY // 2):
                            e.wait_ge(s_pf, u * 4 + (k + 1))
                            for c in range(2):
                                last = nc.tensor.matmul(pp[k][:, 0:D], oh[:, par, 2 * k + c, :],
                                                        ring[:, par, 2 * k + c, :], start=(c == 0), stop=(c == 1))
                            last.then_inc(s_p, 1)
                        e.wait_ge(s_p, u * 4 + 4)
                        e.sem_inc(s_free, 1)
                    steps(e, NBODY, step)

                @blk.vector
                def _(e):
                    L = Link(e, s_v)
                    e.sem_inc(s_pf, 4)
                    L.step(nc.vector.memset(acc[:, 0:T, :], 0.0))

                    def onehot(u, par):
                        e.wait_ge(s_free, u + 1)
                        ins = nc.vector.tensor_tensor(oh[:, par, :, :], bc(iota_row[:, :], 1, BODY),
                                                      bc(lo_s[:, bass.ds(u * BODY, BODY)], 2, P), ALU.is_equal)
                        if w_s is not None:
                            ins.then_inc(s_w, 1)
                            e.wait_ge(s_w, u + 1)
                            ins = nc.vector.tensor_tensor(oh[:, par, :, :], oh[:, par, :, :],
                                                          bc(w_s[:, bass.ds(u * BODY, BODY)], 2, P), ALU.mult)
                        ins.then_inc(s_oh, 1)

                    onehot(0, 0)

                    def step(u, par, i):
                        tl = tiles_of(mybir.EngineType.DVE, u)
                        onehot(u + 1, 1 - par)
                        for k in range(4):
                            e.wait_ge(s_p, u * 4 + (k + 1))
                            e.wait_ge(s_v, u * 4 + (k + 1))
                            a = acc[:, bass.ds(tl[k], 1), 0:D].rearrange("p a d -> p (a d)")
                            nc.vector.tensor_tensor(a, a, pp[k][:, 0:D], ALU.add).then_inc(s_v, 1)
                        e.wait_ge(s_v, u * 4 + 5)
                        e.sem_inc(s_pf, 4)
                    steps(e, NBODY, step)

    KT = 5
    assert T % KT == 0

    def node_products(s, srcs, mm, post, nbank, ndone):
        ns = len(srcs)
        xs = s.sb("xs", [P, KT, ns, D])
        xT = s.sb("xT", [P, KT, ns * D])
        ptr = [s.ps(f"ptr{k}", [P, 512]) for k in range(3)]
        po = [s.ps(f"po{k}", [P, 512]) for k in range(nbank)]
        s_st, s_tr, s_xt, s_mm, s_fr, s_v, s_idle = (s.sem(n) for n in ("st", "tr", "xt", "mm", "fr", "v", "idle"))

        def tview(k):
            return ptr[k % 3][:, 0:ns * D]

        def tensor(e):
            def transposes(k):
                for a in range(ns):
                    for h in range(2):
                        last = nc.tensor.transpose(tview(k)[:, a * D + h * P:a * D + (h + 1) * P],
                                                   xs[:, k, a, h * P:(h + 1) * P], ident[:, :])
                last.then_inc(s_tr, 1)
            e.wait_ge(s_st, 1)
            transposes(0)
            with e.Fori(0, T // KT) as i:
                for k in range(KT):
                    e.wait_ge(s_st, i * KT + (k + 2))
                    transposes((k + 1) % KT)
                    e.wait_ge(s_xt, i * KT + (k + 1))
                    cnt_ = [0, 0]

                    def wait():
                        cnt_[0] += 1
                        e.wait_ge(s_fr, i * (KT * ndone) + (k * ndone + cnt_[0]))

                    def done(ins):
                        cnt_[1] += 1
                        ins.then_inc(s_mm, 1)
                    mm(e, k, po, xT, wait, done)
                    assert cnt_ == [ndone, ndone]

        def scalar(e, extra=None):
            def stage_in(t, k):
                for a, f in enumerate(srcs):
                    last = nc.scalar.copy(xs[:, k, a, :], f(t))
                last.then_inc(s_st, 1)
            if extra:
                extra(e)
            stage_in(0, 0)
            with e.Fori(0, T // KT) as i:
                for k in range(KT):
                    stage_in(i * KT + (k + 1), (k + 1) % KT)
                    e.wait_ge(s_tr, i * KT + (k + 1))
                    nc.scalar.copy(xT[:, k, :], tview(k)).then_inc(s_xt, 1)

        def vector(e, setup=None, fin=None, per=None):
            L = Link(e, s_v, s_idle)
            if setup:
                setup(e, L)
            e.sem_inc(s_fr, credit)
            with L.loop(T // KT, per) as i:
                for k in range(KT):
                    t = i * KT + k
                    def wait(g):
                        e.wait_ge(s_mm, i * (KT * ndone) + (k * ndone + g + 1))

                    def free(n=1):
                        e.sem_inc(s_fr, n)
                    post(e, L, t, k, po, wait, free)
            if fin:
                fin(e, L)
        credit = ndone * nbufs(nbank, ndone)
        return tensor, scalar, vector

    def nbufs(nbank, ndone):
        return KT if nbank == KT else 1

    def layer_norm(dst, mv, g=None, b=None):
        with stage() as s:
            rstd = s.sb("rstd", [P, T])
            shift = s.sb("shift", [P, T])
            split = 17 if g is not None else T
            gb = s.sb("gb", [P, 2, D]) if g is not None else None
            s_a, s_v, s_r, s_n, s_p, s_gb = (s.sem(n) for n in ("a", "v", "r", "n", "p", "gb"))
            with nc.Block() as blk:
                if g is not None:
                    @blk.sync
                    def _(e):
                        e.dma_start(gb[:, 0, :], g.to_broadcast([P, D])).then_inc(s_gb, 16)
                        e.dma_start(gb[:, 1, :], b.to_broadcast([P, D])).then_inc(s_gb, 16)

                    @blk.gpsimd
                    def _(e):
                        rest = dst[:, split:T, :]
                        e.wait_ge(s_gb, 32)
                        e.wait_ge(s_n, T - split)
                        nc.gpsimd.tensor_tensor(rest, rest, bc(gb[:, 0, :], 1, T - split), ALU.mult).then_inc(s_p, 1)
                        e.wait_ge(s_p, 1)
                        nc.gpsimd.tensor_tensor(rest, rest, bc(gb[:, 1, :], 1, T - split), ALU.add)

                @blk.scalar
                def _(e):
                    nc.scalar.activation(rstd[:, :], mv[:, :, 1], ACT.Sqrt, bias=eps_c[:, :]).then_inc(s_a, 1)
                    if split < T:
                        e.wait_ge(s_r, 1)
                    for t in range(split, T):
                        nc.scalar.activation(dst[:, t, :], dst[:, t, :], ACT.Identity, scale=rstd[:, t:t + 1],
                                             bias=shift[:, t:t + 1]).then_inc(s_n, 1)

                @blk.vector
                def _(e):
                    L = Link(e, s_v)
                    e.wait_ge(s_a, 1)
                    L.step(nc.vector.reciprocal(rstd[:, :], rstd[:, :]))
                    if g is None:
                        for t in range(T):
                            L.do(nc.vector.tensor_scalar(dst[:, t, :], dst[:, t, :], mv[:, t, 0:1], rstd[:, t:t + 1],
                                                         ALU.subtract, ALU.mult))
                    else:
                        L.step(nc.vector.scalar_tensor_tensor(shift[:, :], mv[:, :, 0], -1.0, rstd[:, :], ALU.mult, ALU.mult))
                        e.sem_inc(s_r, 1)
                        e.wait_ge(s_gb, 32)
                        first = L.n
                        for t in range(split):
                            L.do(nc.vector.scalar_tensor_tensor(dst[:, t, :], dst[:, t, :], mv[:, t, 0:1], gb[:, 0, :],
                                                                ALU.subtract, ALU.mult))
                        for t in range(split):
                            L.wait(first + t + 1)
                            L.do(nc.vector.scalar_tensor_tensor(dst[:, t, :], dst[:, t, :], rstd[:, t:t + 1], gb[:, 1, :],
                                                                ALU.mult, ALU.add))
                    L.wait()

    mv = keep("mv", [P, T, 2])

    def stats(L, st, dst, t):
        L.alone()
        L.step(nc.vector.bn_stats(st[:, 0:6], dst))
        L.alone()
        L.step(nc.vector.bn_aggr(st[:, 6:8], st[:, 0:6]))
        L.do(nc.vector.tensor_copy(tile(mv, t, 2), st[:, 6:8]))

    def stats_of_five(L, st, a, i):
        L.alone()
        for k in range(KT):
            L.do(nc.vector.bn_stats(st[:, k, 0:6], tile(a, i * KT + k)))
        L.wait()
        L.alone()
        for k in range(KT):
            L.do(nc.vector.bn_aggr(st[:, k, 6:8], st[:, k, 0:6]))
        L.wait()
        L.do(nc.vector.tensor_copy(mv[:, bass.ds(i * KT, KT), :], st[:, :, 6:8]))

    def tile(a, t, w=D):
        return a[:, bass.ds(t, 1), 0:w].rearrange("p a d -> p (a d)")

    def load_kn(e, dst, w, sem):
        e.dma_start(dst, w.rearrange("(h p) m -> p h m", p=P)).then_inc(sem, 16)

    def gnn0():
        sum_edges(src_i, io["x"])
        with stage() as s:
            W = s.sb("W", [P, 2, 2, D])
            st = s.sb("st", [P, 8])
            s_w = s.sem("w")

            def mm(e, k, po, xT, wait, done):
                wait()
                for a in range(2):
                    for h in range(2):
                        last = nc.tensor.matmul(po[k][:, 0:D],
                                                xT[:, k, a * D + h * P:a * D + (h + 1) * P], W[:, a, h, :],
                                                start=(a + h == 0), stop=(a + h == 2))
                done(last)

            def post(e, L, t, k, po, wait, free):
                wait(0)
                L.step(nc.vector.scalar_tensor_tensor(tile(X, t), po[k][:, 0:D], 0.0, tile(X, t), ALU.max, ALU.add))
                free()
                stats(L, st, tile(X, t), t)
                L.wait()
            tens, scal, vec = node_products(s, [lambda t: tile(X, t), lambda t: tile(acc, t)], mm, post, KT, 1)
            with nc.Block() as blk:
                @blk.sync
                def _(e):
                    load_kn(e, W[:, 0, :, :], io["L0_gnn_W"], s_w)
                    load_kn(e, W[:, 1, :, :], io["L0_gnn_M"], s_w)

                @blk.tensor
                def _(e):
                    e.wait_ge(s_w, 32)
                    tens(e)

                blk.scalar(scal)
                blk.vector(lambda e: vec(e, per=4 * KT))
        layer_norm(X, mv)

    def gat_layer(src, dst, W_in, al, ar, b, last_layer):
        with ExitStack() as es:
            Qs = es.enter_context(nc.sbuf_tensor(nc.make_name("Qs", True), [P, T, 3, HD], BF16))
            with stage() as s:
                W = s.sb("W", [P, 2, W8])
                ab = s.sb("ab", [P, 2, D])
                wp = s.sb("wp", [P, D])
                er = s.sb("er", [P, T, HD])
                s_w, s_z, s_o, s_ww = s.sem("w"), s.sem("z"), s.sem("o"), s.sem("ww")

                def mm(e, k, po, xT, wait, done):
                    wait()
                    for h in range(2):
                        last = nc.tensor.matmul(po[k][:, 0:W8], xT[:, k, h * P:(h + 1) * P], W[:, h, :],
                                                start=(h == 0), stop=(h == 1))
                    done(last)

                def post(e, L, t, k, po, wait, free):
                    wait(0)
                    L.step(nc.vector.tensor_copy(tile(acc, t, W8), po[k][:, 0:W8]))
                    free()

                def setup(e, L):
                    e.wait_ge(s_w, 48)
                    for h in range(2):
                        for j in range(2):
                            L.step(nc.vector.tensor_tensor(wp[:, :], W[:, h, 0:D], ab[:, j, :], ALU.mult))
                            L.step(nc.vector.tensor_reduce(W[:, h, D + 4 * j:D + 4 * j + 4],
                                                           wp[:, :].rearrange("p (h x) -> p h x", h=4), AX.X, ALU.add))
                    e.sem_inc(s_ww, 1)

                def fin(e, L):
                    L.step(nc.vector.tensor_copy(er[:, :, :].rearrange("p t (r h) -> p t r h", r=2),
                                                 bc(acc[:, 0:T, D + 4:W8], 2, 2)))
                    L.step(nc.vector.tensor_copy(acc[:, 0:T, D + 4:W8], acc[:, 0:T, D:D + 4]))
                    e.sem_inc(s_z, 1)
                    split3(L, Qs, er)
                tens, scal, vec = node_products(s, [lambda t: tile(src, t)], mm, post, KT, 1)
                with nc.Block() as blk:
                    @blk.sync
                    def _(e):
                        load_kn(e, W[:, :, 0:D], W_in, s_w)
                        for j, a in enumerate((al, ar)):
                            e.dma_start(ab[:, j, :], a.rearrange("h d -> (h d)").unsqueeze(0).to_broadcast([P, D])
                                        ).then_inc(s_w, 16)
                        e.wait_ge(s_z, 1)
                        e.dma_start(tab_z.rearrange("(t p) d -> p t d", p=P), acc[:, 0:T, :]).then_inc(s_o, 16)
                        e.wait_ge(s_o, 16)

                    @blk.tensor
                    def _(e):
                        e.wait_ge(s_ww, 1)
                        tens(e)

                    blk.scalar(scal)
                    blk.vector(lambda e: vec(e, setup=setup, fin=fin, per=KT))
            with nc.sbuf_tensor(nc.make_name("scratch", True), [P, (2 * WC + 3) * P], F32) as scratch:
                attend(Qs, 4, W8, D, src_i, tab_z, scratch)
        with stage() as s:
            r = s.sb("r", [P, T, HD])
            Y = s.sb("Y", [P, 2, KT, D])
            Y0 = s.sb("Y0", [P, 2, KT, D])
            Z = s.sb("Z", [P, 2, KT, D])
            bb = s.sb("bb", [P, D])
            st = s.sb("st", [P, KT, 8])
            s_b, s_v, s_m, s_z, s_a, s_idle = (s.sem(n) for n in ("b", "v", "m", "z", "a", "idle"))
            with nc.Block() as blk:
                @blk.sync
                def _(e):
                    e.dma_start(bb[:, :], b.unsqueeze(0).to_broadcast([P, D])).then_inc(s_b, 16)

                @blk.scalar
                def _(e):
                    def step(u, par, i):
                        e.wait_ge(s_m, u + 1)
                        nc.scalar.activation(Z[:, par, :, :], Y[:, par, :, :], ACT.Relu, scale=-1.0).then_inc(s_z, 1)
                        nc.scalar.activation(Y0[:, par, :, :], Y[:, par, :, :], ACT.Relu)
                        e.wait_ge(s_z, u + 1)
                        nc.scalar.activation(Z[:, par, :, :], Z[:, par, :, :], ACT.Exp, scale=-1.0).then_inc(s_a, 1)
                    steps(e, T // KT, step)

                @blk.vector
                def _(e):
                    L = Link(e, s_v, s_idle)
                    L.step(nc.vector.tensor_scalar(r[:, :, :], acc[:, 0:T, D:W8], 0.5, None, ALU.max))
                    L.step(nc.vector.reciprocal(r[:, :, :], r[:, :, :]))
                    e.wait_ge(s_b, 16)
                    five = lambda a, u, w=D: a[:, bass.ds(u * KT, KT), 0:w]

                    def y_of(u, par):
                        y = Y[:, par, :, :]
                        L.step(nc.vector.tensor_tensor(y.rearrange("p t (h x) -> p t h x", h=4),
                                                       five(acc, u).rearrange("p t (h x) -> p t h x", h=4),
                                                       bc(five(r, u, 4), 3, D // 4), ALU.mult))
                        L.step(nc.vector.tensor_tensor(y, y, five(src, u), ALU.add))
                        L.step(nc.vector.tensor_tensor(y, y, bc(bb[:, :], 1, KT), ALU.add))
                        e.sem_inc(s_m, 1)

                    def elu(u, par):
                        e.wait_ge(s_a, u + 1)
                        o = Y[:, par, :, :] if last_layer else five(dst, u)
                        L.step(nc.vector.scalar_tensor_tensor(o, Z[:, par, :, :], -1.0, Y0[:, par, :, :], ALU.add, ALU.add))
                        if last_layer:
                            L.step(nc.vector.tensor_tensor(five(dst, u), five(dst, u), Y[:, par, :, :], ALU.add))
                            stats_of_five(L, st, dst, u)
                            L.wait()
                    y_of(0, 0)
                    with L.loop(T // KT // 2, 2 * (3 + (3 + 2 * KT if last_layer else 1))) as i:
                        y_of(i * 2 + 1, 1)
                        elu(i * 2, 0)
                        y_of(i * 2 + 2, 0)
                        elu(i * 2 + 1, 1)
                    elu(T // KT - 1, 0)

    def split3(L, Qs, q):
        for r in range(3):
            L.step(nc.vector.tensor_copy(Qs[:, :, r, :], q[:, :, :]))
            if r < 2:
                L.step(nc.vector.tensor_tensor(q[:, :, :], q[:, :, :], Qs[:, :, r, :], ALU.subtract))

    def gnn1():
        gat_layer(X, H, io["L1_gnn_W0"], io["L1_gnn_al0"], io["L1_gnn_ar0"], io["L1_gnn_b0"], False)
        gat_layer(H, X, io["L1_gnn_W1"], io["L1_gnn_al1"], io["L1_gnn_ar1"], io["L1_gnn_b1"], True)
        layer_norm(X, mv)

    NE, HW = 3, D // HD
    KW = (2 + NE) * HW
    HALFS = range(2)

    def gnn2_tables(l, Qs):
        with ExitStack() as es:
            W = es.enter_context(nc.sbuf_tensor(nc.make_name("Wt", True), [P, HD, KW], F32))
            with stage() as s:
                WK = s.sb("WK", [P, HD, HW])
                WKT = s.sb("WKT", [HW, HD, P])
                WE = s.sb("WE", [HW, NE, HD, HW])
                mus = s.sb("mus", [P, HD, NE])
                pk = [s.ps(f"pk{k}", [P, 512]) for k in range(2)]
                pm = [s.ps(f"pm{k}", [P, 512]) for k in range(2)]
                s_w, s_t, s_e, s_m, s_v = (s.sem(n) for n in ("w", "t", "e", "m", "v"))
                n_loads = 3 * NT + NE + 1
                with nc.Block() as blk:
                    @blk.sync
                    def _(e):
                        for t in range(NT):
                            rows = slice(t * HW, (t + 1) * HW)
                            for name, o in (("W_K", WK[rows, :, :]), ("W_Q", W[rows, :, 0:HW]), ("W_V", W[rows, :, HW:2 * HW])):
                                e.dma_start(o, io["L2_gnn_" + name][bass.ds(l, 1), t, :, :, :].rearrange("o h d x -> d (o h) x")
                                            ).then_inc(s_w, 16)
                        for t in range(NE):
                            e.dma_start(WE[:, t, :, :], io["L2_gnn_W_E"][bass.ds(l, 1), t, :, :, :].rearrange("o h d x -> d (o h) x")
                                        ).then_inc(s_w, 16)
                        e.dma_start(mus[:, :, :].rearrange("p h t -> p (h t)"),
                                    io["L2_gnn_mu"][bass.ds(l, 1), :, :].rearrange("o h t -> o (h t)").to_broadcast([P, HD * NE])
                                    ).then_inc(s_w, 16)
                        e.wait_ge(s_w, 16 * n_loads)

                    @blk.tensor
                    def _(e):
                        e.wait_ge(s_w, 16 * n_loads)
                        for h in range(HD):
                            last = nc.tensor.transpose(pk[h // 4][0:HW, (h % 4) * P:(h % 4 + 1) * P], WK[:, h, :], ident[:, :])
                            if h % 4 == 3:
                                last.then_inc(s_t, 1)
                        e.wait_ge(s_e, 2)
                        for h in range(HD):
                            last = nc.tensor.matmul(pm[h // 4][:, (h % 4) * P:(h % 4) * P + NE * HW], WKT[:, h, :], WE[:, :, h, :],
                                                    start=True, stop=True)
                            if h % 4 == 3:
                                last.then_inc(s_m, 1)

                    @blk.scalar
                    def _(e):
                        for k in range(2):
                            e.wait_ge(s_t, k + 1)
                            nc.scalar.copy(WKT[:, 4 * k:4 * k + 4, :].rearrange("p j x -> p (j x)"), pk[k][0:HW, :]).then_inc(s_e, 1)

                    @blk.vector
                    def _(e):
                        L = Link(e, s_v)
                        e.wait_ge(s_w, 16 * n_loads)
                        L.step(nc.vector.tensor_scalar(mus[:, :, :], mus[:, :, :], float(HW) ** -0.5, None, ALU.mult))
                        for k in range(2):
                            e.wait_ge(s_m, k + 1)
                            L.do(nc.vector.tensor_tensor(
                                W[:, 4 * k:4 * k + 4, 2 * HW:KW].rearrange("p h (t x) -> p h t x", t=NE),
                                pm[k][:, :].rearrange("p (h y) -> p h y", h=4)[:, :, 0:NE * HW].rearrange("p h (t x) -> p h t x", t=NE),
                                bc(mus[:, 4 * k:4 * k + 4, :], 3, HW), ALU.mult))
            with stage() as s:
                xm = s.sb("xm", [P, 2, HD, NT, HW])
                xT = s.sb("xT", [P, 2, HD, P])
                kv = acc[:, :, :].rearrange("p t d -> p (t d)")[:, 0:2 * (1 + NE) * D].rearrange("p (b c h x) -> p b c h x", b=2, h=HD, x=HW)
                q = s.sb("q", [P, 2, HD, HW])
                pT = [[s.ps(f"pT{b}{k}", [P, 512]) for k in range(2)] for b in range(2)]
                po = [s.ps(f"po{k}", [P, 512]) for k in range(3)]
                banks = [range(0, 3), range(3, 6), range(6, 8)]
                s_xm, s_tr, s_xt, s_mm, s_kv, s_q, s_ko, s_idle, s_v = (
                    s.sem(n) for n in ("xm", "tr", "xt", "mm", "kv", "q", "ko", "idle", "v"))
                s_o = [s.sem("o0"), s.sem("o1")]

                def heads_of(k, a, b):
                    n = len(banks[k])
                    return po[k][:, 0:n * KW].rearrange("p (h c) -> p h c", c=KW)[:, :, a:b]

                with nc.Block() as blk:
                    @blk.gpsimd
                    def _(e):
                        def step(t, par, i):
                            e.wait_ge(s_tr, t + 1)
                            e.sem_inc(s_idle, 1)
                            nc.gpsimd.tensor_tensor(
                                xm[:, par, :, :, :], bc(tile(H, t).rearrange("p (h x) -> p h x", h=HD), 2, NT),
                                bc(bc(masks[:, bass.ds(t, 1), :].rearrange("p a m -> p (a m)"), 1, HD), 3, HW), ALU.mult
                                ).then_inc(s_xm, 1)
                        steps(e, T, step)

                    @blk.tensor
                    def _(e):
                        e.sem_inc(s_tr, 2)

                        def transposes(t, par):
                            e.wait_ge(s_xm, t + 1)
                            for h in range(HD):
                                last = nc.tensor.transpose(pT[par][h // 4][:, (h % 4) * P:(h % 4 + 1) * P],
                                                           xm[:, par, h, :, :].rearrange("p m x -> p (m x)"), ident[:, :])
                            last.then_inc(s_tr, 1)

                        def products(t, par):
                            e.wait_ge(s_xt, t + 1)
                            for k, hs in enumerate(banks):
                                e.wait_ge(s_kv, t * 3 + (k + 1))
                                e.wait_ge(s_q, t * 3 + (k + 1))
                                for j, h in enumerate(hs):
                                    last = nc.tensor.matmul(po[k][:, j * KW:(j + 1) * KW], xT[:, par, h, :], W[:, h, :],
                                                            start=True, stop=True)
                                last.then_inc(s_mm, 1)
                        transposes(0, 0)
                        with e.Fori(0, T // 2) as i:
                            transposes(i * 2 + 1, 1)
                            products(i * 2, 0)
                            transposes(i * 2 + 2, 0)
                            products(i * 2 + 1, 1)
                        products(T - 1, 0)

                    @blk.scalar
                    def _(e):
                        e.sem_inc(s_kv, 3)

                        def evacuate(t, par):
                            e.wait_ge(s_tr, t + 3)
                            for k in range(2):
                                last = nc.scalar.copy(xT[:, par, 4 * k:4 * k + 4, :].rearrange("p h n -> p (h n)"), pT[par][k][:, :])
                            last.then_inc(s_xt, 1)

                        def rows(t, par):
                            e.wait_ge(s_ko, t + 1)
                            for k, hs in enumerate(banks):
                                e.wait_ge(s_mm, t * 3 + (k + 1))
                                nc.scalar.copy(kv[:, par, :, hs[0]:hs[-1] + 1, :].rearrange("p c h x -> p h c x"),
                                               heads_of(k, HW, KW).rearrange("p h (c x) -> p h c x", x=HW)).then_inc(s_kv, 1)
                        evacuate(0, 0)
                        with e.Fori(0, T // 2) as i:
                            evacuate(i * 2 + 1, 1)
                            rows(i * 2, 0)
                            evacuate(i * 2 + 2, 0)
                            rows(i * 2 + 1, 1)
                        rows(T - 1, 0)

                    @blk.vector
                    def _(e):
                        L = Link(e, s_v)
                        e.sem_inc(s_q, 3)

                        def step(t, par, i):
                            L.i, L.per, L.n = t, 4, 0
                            for k, hs in enumerate(banks):
                                e.wait_ge(s_kv, t * 3 + (k + 4))
                                nc.vector.tensor_copy(q[:, 0, hs[0]:hs[-1] + 1, :], heads_of(k, 0, HW)).then_inc(s_q, 1)
                            e.wait_ge(s_q, t * 3 + 6)
                            Qt = Qs[:, bass.ds(t, 1), :, :].rearrange("p a r d -> p (a r) d")
                            q0, q1 = (q[:, b, :, :].rearrange("p h x -> p (h x)") for b in range(2))
                            L.step(nc.vector.tensor_copy(Qt[:, 0, :], q0))
                            L.step(nc.vector.tensor_tensor(q1, q0, Qt[:, 0, :], ALU.subtract))
                            L.step(nc.vector.tensor_copy(Qt[:, 1, :], q1))
                            L.do(nc.vector.tensor_tensor(Qt[:, 2, :], q1, Qt[:, 1, :], ALU.subtract))
                            L.wait()
                        steps(e, T, step)

                    @blk.sync
                    def _(e):
                        e.sem_inc(s_ko, 1)
                        t_v = tab_kv.rearrange("(s t p) c -> p s t c", s=NE, p=P)

                        def out_rows(t, par):
                            e.wait_ge(s_kv, t * 3 + 6)
                            o = t_v[:, :, bass.ds(t, 1), :].rearrange("p s t c -> p s (t c)")
                            st = kv[:, par, :, :, :].rearrange("p c h x -> p c (h x)")
                            e.dma_start(o[:, :, 0:D], bc(st[:, 0, :], 1, NE)).then_inc(s_o[par], 16)
                            e.dma_start(o[:, :, D:2 * D], st[:, 1:, :]).then_inc(s_o[par], 16)
                        out_rows(0, 0)
                        e.sem_inc(s_ko, 1)
                        with e.Fori(0, T // 2) as i:
                            out_rows(i * 2 + 1, 1)
                            e.wait_ge(s_o[0], i * 32 + 32)
                            e.sem_inc(s_ko, 1)
                            out_rows(i * 2 + 2, 0)
                            e.wait_ge(s_o[1], i * 32 + 32)
                            e.sem_inc(s_ko, 1)
                        e.wait_ge(s_o[0], 32 * (T // 2 + 1))

    def gnn2_layer(l):
        row = lambda name: io["L2_gnn_" + name][bass.ds(l, 1), :]
        with ExitStack() as es:
            Qs = es.enter_context(nc.sbuf_tensor(nc.make_name("Qs", True), [P, T, 3, D], BF16))
            gnn2_tables(l, Qs)
            attend(Qs, HD, 2 * D, D, idx3_i, tab_kv, X[:, :, :].rearrange("p t d -> p (t d)"))
        with stage() as s:
            W = s.sb("W", [P, 2, D])
            r = s.sb("r", [P, T, HD])
            bo = s.sb("bo", [P, D])
            st = s.sb("st", [P, KT, 8])
            s_w, s_b, s_n = s.sem("w"), s.sem("b"), s.sem("n")

            def mm(e, k, po, xT, wait, done):
                wait()
                for h in HALFS:
                    last = nc.tensor.matmul(po[k][:, 0:D], xT[:, k, h * P:(h + 1) * P], W[:, h, :],
                                            start=(h == 0), stop=(h == 1))
                done(last)

            def setup(e, L):
                L.step(nc.vector.tensor_scalar(r[:, :, :], acc[:, 0:T, D:W8], 1e-10, None, ALU.add))
                L.step(nc.vector.reciprocal(r[:, :, :], r[:, :, :]))
                av = acc[:, 0:T, 0:D].rearrange("p t (h x) -> p t h x", h=HD)
                L.step(nc.vector.tensor_tensor(av, av, bc(r[:, :, :], 3, HW), ALU.mult))
                e.sem_inc(s_n, 1)
                e.wait_ge(s_b, 16)
                L.step(nc.vector.tensor_tensor(H[:, 0:T, :], H[:, 0:T, :], bc(bo[:, :], 1, T), ALU.add))

            def post(e, L, t, k, po, wait, free):
                wait(0)
                L.step(nc.vector.scalar_tensor_tensor(tile(H, t), po[k][:, 0:D], 1.0, tile(H, t), ALU.mult, ALU.add))
                free()
                if k == KT - 1:
                    stats_of_five(L, st, H, L.i)
                    L.wait()
            tens, scal, vec = node_products(s, [lambda t: tile(acc, t)], mm, post, KT, 1)
            with nc.Block() as blk:
                @blk.sync
                def _(e):
                    e.dma_start(W[:, :, :], io["L2_gnn_Wo"][bass.ds(l, 1), :, :].rearrange("o (h p) m -> p (o h) m", p=P)
                                ).then_inc(s_w, 16)
                    e.dma_start(bo[:, :], row("bo").to_broadcast([P, D])).then_inc(s_b, 16)

                @blk.tensor
                def _(e):
                    e.wait_ge(s_w, 16)
                    tens(e)

                @blk.scalar
                def _(e):
                    scal(e, extra=lambda e: e.wait_ge(s_n, 1))

                blk.vector(lambda e: vec(e, setup=setup, per=KT + 2 * KT + 1))
        layer_norm(H, mv, row("ln1_g"), row("ln1_b"))
        FB = 4 * D // P
        with stage() as s:
            w1 = s.sb("w1", [P, 2, 4 * D])
            w2 = s.sb("w2", [P, FB, D])
            b1 = s.sb("b1", [P, FB])
            b2 = s.sb("b2", [P, D])
            xs = s.sb("xs", [P, KT, D])
            xT = s.sb("xT", [P, KT, D])
            hT = s.sb("hT", [P, 2, 4, P])
            st = s.sb("st", [P, 8])
            ptr = [s.ps(f"ptr{k}", [P, 512]) for k in range(3)]
            ph = [s.ps(f"ph{k}", [P, 512]) for k in range(2)]
            po = [s.ps(f"po{k}", [P, 512]) for k in range(3)]
            s_w, s_st, s_tr, s_xt, s_h, s_g, s_o, s_fr, s_v, s_idle = (
                s.sem(n) for n in ("w", "st", "tr", "xt", "h", "g", "o", "fr", "v", "idle"))
            with nc.Block() as blk:
                @blk.sync
                def _(e):
                    e.dma_start(w1[:, :, :], io["L2_gnn_w1"][bass.ds(l, 1), :, :].rearrange("o (h p) m -> p (o h) m", p=P)
                                ).then_inc(s_w, 16)
                    e.dma_start(w2[:, :, :], io["L2_gnn_w2"][bass.ds(l, 1), :, :].rearrange("o (f p) m -> p (o f) m", p=P)
                                ).then_inc(s_w, 16)
                    with nc.allow_non_contiguous_dma(reason="1024 words"):
                        e.dma_start(b1[:, :], row("b1").rearrange("o (f p) -> p (o f)", p=P)).then_inc(s_w, 16)
                    e.dma_start(b2[:, :], row("b2").to_broadcast([P, D])).then_inc(s_w, 16)

                @blk.tensor
                def _(e):
                    def transposes(k):
                        for h in HALFS:
                            last = nc.tensor.transpose(ptr[k % 3][:, h * P:(h + 1) * P], xs[:, k, h * P:(h + 1) * P], ident[:, :])
                        last.then_inc(s_tr, 1)
                    e.wait_ge(s_w, 64)
                    e.wait_ge(s_st, 1)
                    transposes(0)
                    with e.Fori(0, T // KT) as i:
                        for k in range(KT):
                            e.wait_ge(s_st, i * KT + (k + 2))
                            transposes((k + 1) % KT)
                            e.wait_ge(s_xt, i * KT + (k + 1))
                            for g in range(2):
                                for f in range(4):
                                    for h in HALFS:
                                        fb = 4 * g + f
                                        last = nc.tensor.matmul(ph[g][:, f * P:(f + 1) * P], w1[:, h, fb * P:(fb + 1) * P],
                                                                xT[:, k, h * P:(h + 1) * P], start=(h == 0), stop=(h == 1))
                                last.then_inc(s_h, 1)
                            e.wait_ge(s_fr, i * KT + (k + 1))
                            for g in range(2):
                                e.wait_ge(s_g, i * (2 * KT) + (2 * k + g + 1))
                                for f in range(4):
                                    last = nc.tensor.matmul(po[k % 3][:, 0:D], hT[:, g, f, :], w2[:, 4 * g + f, :],
                                                            start=(g + f == 0), stop=(g + f == 4))
                            last.then_inc(s_o, 1)

                @blk.scalar
                def _(e):
                    def stage_in(t, k):
                        nc.scalar.copy(xs[:, k, :], tile(H, t)).then_inc(s_st, 1)
                    e.wait_ge(s_w, 64)
                    stage_in(0, 0)
                    with e.Fori(0, T // KT) as i:
                        for k in range(KT):
                            stage_in(i * KT + (k + 1), (k + 1) % KT)
                            e.wait_ge(s_tr, i * KT + (k + 1))
                            nc.scalar.copy(xT[:, k, :], ptr[k % 3][:, 0:D]).then_inc(s_xt, 1)
                            for g in range(2):
                                e.wait_ge(s_h, i * (2 * KT) + (2 * k + g + 1))
                                for f in range(4):
                                    last = nc.scalar.activation(hT[:, g, f, :], ph[g][:, f * P:(f + 1) * P], ACT.Gelu,
                                                                bias=b1[:, 4 * g + f:4 * g + f + 1])
                                last.then_inc(s_g, 1)

                @blk.vector
                def _(e):
                    L = Link(e, s_v, s_idle)
                    e.wait_ge(s_w, 64)
                    e.sem_inc(s_fr, 2)
                    with L.loop(T // KT, 5 * KT) as i:
                        for k in range(KT):
                            t = i * KT + k
                            e.wait_ge(s_o, t + 1)
                            L.step(nc.vector.scalar_tensor_tensor(tile(H, t), po[k % 3][:, 0:D], 1.0, tile(H, t),
                                                                  ALU.mult, ALU.add))
                            e.sem_inc(s_fr, 1)
                            L.step(nc.vector.tensor_tensor(tile(H, t), tile(H, t), b2[:, :], ALU.add))
                            stats(L, st, tile(H, t), t)
                            L.wait()
        layer_norm(H, mv, row("ln2_g"), row("ln2_b"))

    def gnn2():
        copy_tiles(H, X, keep_x, True)
        with nc.Fori(0, 3) as l:
            gnn2_layer(l)
        copy_tiles(None, X, keep_x, False)
        tile_stats(H)
        layer_norm(H, mv, io["L2_gnn_out_g"].unsqueeze(0), io["L2_gnn_out_b"].unsqueeze(0))
        add_stats(X, H)
        layer_norm(X, mv)

    def copy_tiles(dst, src, dram, out_):
        with stage() as s:
            s_o = s.sem("o")
            with nc.Block() as blk:
                @blk.sync
                def _(e):
                    a = src[:, 0:T, :].rearrange("p t d -> p (t d)")
                    e.dma_start(*((dram, a) if out_ else (a, dram))).then_inc(s_o, 16)
                    e.wait_ge(s_o, 16)

                if dst is not None:
                    @blk.vector
                    def _(e):
                        nc.vector.tensor_copy(dst[:, 0:T, :], src[:, 0:T, :])

    def tile_stats(a):
        add_stats(a, None)

    def add_stats(a, b):
        with stage() as s:
            st = s.sb("st", [P, KT, 8])
            s_v, s_idle = s.sem("v"), s.sem("idle")
            with nc.Block() as blk:
                @blk.vector
                def _(e):
                    L = Link(e, s_v, s_idle)
                    with L.loop(T // KT, 2 * KT + (2 if b is not None else 1)) as i:
                        ts = bass.ds(i * KT, KT)
                        if b is not None:
                            L.step(nc.vector.tensor_tensor(a[:, ts, :], a[:, ts, :], b[:, ts, 0:D], ALU.add))
                        stats_of_five(L, st, a, i)
                        L.wait()

    def gnn3():
        NR = 8
        with stage() as s:
            W = s.sb("W", [P, 2, NR, P])
            hs = acc[:, :, :].rearrange("p t d -> p (t d)")[:, 0:3 * NR * D].rearrange("p (k h c) -> p k h c", k=3, h=2)
            buf = [0, 1, 2, 0, 1]
            s_z, s_w, s_c, s_ho = s.sem("z"), s.sem("w"), s.sem("c"), s.sem("ho")
            s_o = s.sem("o")

            def mm(e, k, po, xT, wait, done):
                for h in HALFS:
                    wait()
                    for j in range(2):
                        last = nc.tensor.matmul(po[2 * h + j][:, :], xT[:, k, h * P:(h + 1) * P],
                                                W[:, h, 4 * j:4 * j + 4, :].rearrange("p r x -> p (r x)"), start=True, stop=True)
                    done(last)

            def post(e, L, t, k, po, wait, free):
                e.wait_ge(s_ho, t + 1)
                for h in HALFS:
                    wait(h)
                    for j in range(2):
                        L.do(nc.vector.tensor_copy(hs[:, buf[k], h, j * 512:(j + 1) * 512], po[2 * h + j][:, :]))
                    L.wait()
                    free()
                e.sem_inc(s_c, 1)
            tens, scal, vec = node_products(s, [lambda t: tile(X, t)], mm, post, 4, 2)
            with nc.Block() as blk:
                @blk.sync
                def _(e):
                    e.wait_ge(s_z, 1)
                    for q in range(4):
                        for h in HALFS:
                            a = io["L3_gnn_weight"].rearrange("r (b i o) -> b i r o", b=HD, i=HW)[4 * h + q]
                            e.dma_start(W[q * HW:(q + 1) * HW, h, :, q * HW:(q + 1) * HW], a).then_inc(s_w, 16)
                    e.sem_inc(s_ho, 2)
                    h_v = tab_h.rearrange("(r t p) (h x) -> p h r t x", r=NR, p=P, h=2)
                    with e.Fori(0, T // KT) as i:
                        for k in range(KT):
                            e.wait_ge(s_c, i * KT + (k + 1))
                            for h in HALFS:
                                e.dma_start(h_v[:, h, :, bass.ds(i * KT + k, 1), :].rearrange("p r t x -> p r (t x)"),
                                            hs[:, buf[k], h, :].rearrange("p (r x) -> p r x", r=NR)).then_inc(s_o, 16)
                            e.wait_ge(s_o, i * (32 * KT) + (32 * k + 32))
                            e.sem_inc(s_ho, 1)

                @blk.gpsimd
                def _(e):
                    nc.gpsimd.memset(W[:, :, :, :], 0.0).then_inc(s_z, 1)

                @blk.tensor
                def _(e):
                    e.wait_ge(s_w, 128)
                    tens(e)

                blk.scalar(scal)
                blk.vector(lambda e: vec(e, per=4 * KT))
        with ExitStack() as es:
            idx8_i = es.enter_context(nc.sbuf_tensor("idx8_i", [P, CH], I32))
            w_s = es.enter_context(nc.sbuf_tensor("w_s", [P, CH + BODY], F32))
            with stage() as s:
                s_l = s.sem("l")
                with nc.Block() as blk:
                    @blk.vector
                    def _(e):
                        nc.vector.memset(w_s[:, CH:], 0.0)

                    @blk.sync
                    def _(e):
                        e.dma_start(idx8_i[:, :], keep_i8).then_inc(s_l, 16)
                        e.dma_start(w_s[:, 0:CH], keep_w).then_inc(s_l, 16)
                        e.wait_ge(s_l, 32)
            sum_edges(idx8_i, tab_h, w_s)
        add_stats(X, acc)
        layer_norm(X, mv)
        with stage() as s:
            s_o = s.sem("o")
            with nc.Block() as blk:
                @blk.sync
                def _(e):
                    e.dma_start(out[0:(T - 1) * P, :].rearrange("(t p) d -> p t d", p=P), X[:, 0:T - 1, :]).then_inc(s_o, 16)
                    e.dma_start(out[(T - 1) * P:N, :], X[0:TAIL, T - 1, :]).then_inc(s_o, 16)
                    e.wait_ge(s_o, 32)

    gnn0()
    gnn1()
    gnn2()
    gnn3()

    outer.close()


_INS = ["x", "src", "dst", "edge_type_3", "edge_type_8", "edge_weight", "node_type_4", "L0_gnn_W", "L0_gnn_M",
        "L1_gnn_W0", "L1_gnn_al0", "L1_gnn_ar0", "L1_gnn_b0", "L1_gnn_W1", "L1_gnn_al1", "L1_gnn_ar1", "L1_gnn_b1",
        "L2_gnn_W_Q", "L2_gnn_W_K", "L2_gnn_W_V", "L2_gnn_W_E", "L2_gnn_mu", "L2_gnn_Wo", "L2_gnn_bo",
        "L2_gnn_ln1_g", "L2_gnn_ln1_b", "L2_gnn_ln2_g", "L2_gnn_ln2_b", "L2_gnn_w1", "L2_gnn_b1", "L2_gnn_w2",
        "L2_gnn_b2", "L2_gnn_out_g", "L2_gnn_out_b", "L3_gnn_weight"]


def kernel(**inputs):
    import concourse.bacc as _bacc
    from concourse.bass_utils import run_bass_kernel_spmd as _run

    nc = _bacc.Bacc("TRN2", target_bir_lowering=False, num_devices=1)
    arrays, io = {}, {}
    for name in _INS:
        a = np.ascontiguousarray(inputs[name])
        arrays[f"in_{name}"] = a
        io[name] = nc.dram_tensor(f"in_{name}", a.shape, mybir.dt.from_np(a.dtype), kind="ExternalInput").ap()
    io["out"] = nc.dram_tensor("out_0", (N, D), F32, kind="ExternalOutput").ap()
    build(nc, io)
    r = _run(nc, [arrays], core_ids=[0])
    return r.results[0]["out_0"]
```
